# Optimizing a Trainium2 kernel written in Bass

```python
import numpy as np
import jax
import jax.numpy as jnp

def _softmax(x, axis=-1):
    return jax.nn.softmax(x, axis=axis)

def _gelu(x):
    return jax.nn.gelu(x, approximate=True)

def _silu(x):
    return jax.nn.silu(x)

def _sigmoid(x):
    return jax.nn.sigmoid(x)

def _layernorm(x, axis=-1, eps=1e-05):
    m = jnp.mean(x, axis=axis, keepdims=True)
    v = jnp.var(x, axis=axis, keepdims=True)
    return (x - m) / jnp.sqrt(v + eps)

def _scatter_add(tgt, idx, src, axis=0):
    return tgt.at[idx].add(src)

def _segment_sum(src, seg, n):
    return jax.ops.segment_sum(src, seg, n)
kernel_name = 'mk_gnn_preln_d1_gnn_r32_be3610'

def setup_inputs(seed: int=0):
    np.random.seed(seed)
    _w = jnp.asarray

    def _rec_inputs():
        import jax
        import jax.numpy as jnp
        _gk = jax.random.key(seed)
        x = -0.000202 + 1 * jax.random.normal(jax.random.fold_in(_gk, 1), (50000, 128), jnp.float32)
        src = jax.random.randint(jax.random.fold_in(_gk, 2), (25000,), 0, 50000, jnp.int32)
        dst = jnp.minimum((50000 * jax.random.uniform(jax.random.fold_in(_gk, 3), (25000,)) ** 2.0).astype(jnp.int32), 49999)
        _o = jnp.argsort(dst, stable=True)
        src = src[_o]
        dst = dst[_o]
        edge_attr_128 = 4.59472e-05 + 1.00006 * jax.random.normal(jax.random.fold_in(_gk, 11), (25000, 128), jnp.float32)
        return (x, src, dst, edge_attr_128)
    x, src, dst, edge_attr_128 = _rec_inputs()

    def _L0_gnn_setup():
        import jax, jax.numpy as jnp
        import numpy as np
        N = 50000
        E = 625000
        D = 128
        DF = 4 * D

        def layernorm(x, gamma, beta, eps=1e-05):
            mu = jnp.mean(x, axis=-1, keepdims=True)
            var = jnp.var(x, axis=-1, keepdims=True)
            return (x - mu) * jax.lax.rsqrt(var + eps) * gamma + beta
        key = jax.random.key(seed)
        ks = jax.random.split(key, 12)
        s = 1.0 / np.sqrt(D)
        sf = 1.0 / np.sqrt(DF)
        return {'x': jax.random.normal(ks[0], (N, D), jnp.float32), 'edge_index': jax.random.randint(ks[1], (2, E), 0, N, jnp.int32), 'edge_attr': jax.random.normal(ks[2], (E, D), jnp.float32), 'g1': jnp.ones((D,), jnp.float32), 'b1': jnp.zeros((D,), jnp.float32), 'g2': jnp.ones((D,), jnp.float32), 'b2': jnp.zeros((D,), jnp.float32), 'eps_gin': jnp.zeros((), jnp.float32), 'Wg1': jax.random.uniform(ks[3], (D, D), jnp.float32, -s, s), 'bg1': jnp.zeros((D,), jnp.float32), 'Wg2': jax.random.uniform(ks[4], (D, D), jnp.float32, -s, s), 'bg2': jnp.zeros((D,), jnp.float32), 'Wf1': jax.random.uniform(ks[5], (D, DF), jnp.float32, -s, s), 'bf1': jnp.zeros((DF,), jnp.float32), 'Wf2': jax.random.uniform(ks[6], (DF, D), jnp.float32, -sf, sf), 'bf2': jnp.zeros((D,), jnp.float32)}
    _L0_gnn_all = _L0_gnn_setup()
    _L0_gnn_in = {k: v for k, v in _L0_gnn_all.items() if k in ('g1', 'b1', 'g2', 'b2', 'eps_gin', 'Wg1', 'bg1', 'Wg2', 'bg2', 'Wf1', 'bf1', 'Wf2', 'bf2')}
    del _L0_gnn_all
    return {'x': x, 'src': src, 'dst': dst, 'edge_attr_128': edge_attr_128, 'L0_gnn_g1': _L0_gnn_in['g1'], 'L0_gnn_b1': _L0_gnn_in['b1'], 'L0_gnn_g2': _L0_gnn_in['g2'], 'L0_gnn_b2': _L0_gnn_in['b2'], 'L0_gnn_eps_gin': _L0_gnn_in['eps_gin'], 'L0_gnn_Wg1': _L0_gnn_in['Wg1'], 'L0_gnn_bg1': _L0_gnn_in['bg1'], 'L0_gnn_Wg2': _L0_gnn_in['Wg2'], 'L0_gnn_bg2': _L0_gnn_in['bg2'], 'L0_gnn_Wf1': _L0_gnn_in['Wf1'], 'L0_gnn_bf1': _L0_gnn_in['bf1'], 'L0_gnn_Wf2': _L0_gnn_in['Wf2'], 'L0_gnn_bf2': _L0_gnn_in['bf2']}

def reference(x, src, dst, edge_attr_128, L0_gnn_g1, L0_gnn_b1, L0_gnn_g2, L0_gnn_b2, L0_gnn_eps_gin, L0_gnn_Wg1, L0_gnn_bg1, L0_gnn_Wg2, L0_gnn_bg2, L0_gnn_Wf1, L0_gnn_bf1, L0_gnn_Wf2, L0_gnn_bf2):
    import jax
    import jax.numpy as jnp

    def _L0_gnn_ref(x, edge_index, edge_attr, g1, b1, g2, b2, eps_gin, Wg1, bg1, Wg2, bg2, Wf1, bf1, Wf2, bf2):
        import jax, jax.numpy as jnp
        import numpy as np
        N = 50000
        E = 625000
        D = 128
        DF = 4 * D

        def layernorm(x, gamma, beta, eps=1e-05):
            mu = jnp.mean(x, axis=-1, keepdims=True)
            var = jnp.var(x, axis=-1, keepdims=True)
            return (x - mu) * jax.lax.rsqrt(var + eps) * gamma + beta
        src = edge_index[0]
        dst = edge_index[1]
        xn = layernorm(x, g1, b1)
        msg = jax.nn.relu(xn[src] + edge_attr)
        aggr = jax.ops.segment_sum(msg, dst, num_segments=N)
        h = (1.0 + eps_gin) * xn + aggr
        h = jax.nn.relu(h @ Wg1 + bg1) @ Wg2 + bg2
        x = x + h
        xn2 = layernorm(x, g2, b2)
        f = jax.nn.gelu(xn2 @ Wf1 + bf1, approximate=False) @ Wf2 + bf2
        return x + f
    edge_index = jnp.stack([src, dst])
    h = jnp.maximum(_layernorm(x, axis=-1), 0.0)
    x = x + _L0_gnn_ref(h, edge_index, edge_attr_128, L0_gnn_g1, L0_gnn_b1, L0_gnn_g2, L0_gnn_b2, L0_gnn_eps_gin, L0_gnn_Wg1, L0_gnn_bg1, L0_gnn_Wg2, L0_gnn_bg2, L0_gnn_Wf1, L0_gnn_bf1, L0_gnn_Wf2, L0_gnn_bf2)
    return x

_drawn_inputs = setup_inputs


def setup_inputs(seed=0):
    import zlib

    import numpy as np

    out = dict(_drawn_inputs(seed))
    spreads = {'L0_gnn_g1': (1.0, 0.2),
     'L0_gnn_b1': (0.0, 0.418),
     'L0_gnn_g2': (1.0, 0.6),
     'L0_gnn_b2': (0.0, 0.687),
     'L0_gnn_bg1': (0.0, 0.331),
     'L0_gnn_bg2': (0.0, 0.1),
     'L0_gnn_bf1': (0.0, 0.375),
     'L0_gnn_bf2': (0.0, 0.1)}
    factors = {}
    for name, (base, spread) in spreads.items():
        noise = np.random.default_rng([zlib.crc32(name.encode()), seed]).standard_normal(out[name].shape)
        drawn = base * np.exp(spread * noise) if base else spread * noise
        out[name] = jnp.asarray(drawn.astype(out[name].dtype))
    for name, factor in factors.items():
        out[name] = (out[name] * factor).astype(out[name].dtype)
    return out
```

```python
from contextlib import ExitStack

import concourse.bass as bass
from concourse import mybir

ALU = mybir.AluOpType
ACT = mybir.ActivationFunctionType
F32 = mybir.dt.float32
I32 = mybir.dt.int32

P = 128
J = 4
BLOCK = P * J
RING = 4
EPS = 1e-5


class Item:

    def __init__(self, at, turn, slot, rows):
        self.at, self.turn, self.slot, self.rows = at, turn, slot, rows


def pipeline(eng, count, tail_rows, lag, step):

    def peeled(t):
        def item_of(o):
            b = t - o
            if b < 0 or b >= count:
                return None
            return Item(b, b // RING, b % RING, tail_rows if b == count - 1 else P)
        step(item_of)

    first = -(-(lag + RING) // RING)
    last = (count - 1) // RING
    for t in range(first * RING):
        peeled(t)
    with eng.Fori(first, last) as n:
        for k in range(RING):
            def item_of(o, k=k):
                return Item(n * RING + (k - o), n + (k - o) // RING, (k - o) % RING, P)
            step(item_of)
    for t in range(last * RING, count + lag):
        peeled(t)


def reached(eng, sem, value):
    if isinstance(value, int) and value <= 0:
        return
    eng.wait_ge(sem, value)


def gnn_kernel(nc, x, edge_attr, edge_cols, dst_rows, g1, b1, g2, b2, eps_gin,
               Wg1, bg1, Wg2, bg2, Wf1, bf1, Wf2, bf2, out):
    N, D = x.shape
    E = edge_attr.shape[0]
    DF = Wf1.shape[1]
    KF = DF // P
    NB, NC = -(-N // BLOCK), -(-E // BLOCK)
    NB_TAIL, NC_TAIL = (N - (NB - 1) * BLOCK) // J, (E - (NC - 1) * BLOCK) // J
    assert D == P and NB_TAIL * J + (NB - 1) * BLOCK == N and NC_TAIL * J + (NC - 1) * BLOCK == E

    SPARE = N + BLOCK
    ZERO_W = 1024
    AGGR_ROWS = -(-SPARE // ZERO_W) * ZERO_W
    aggr = nc.dram_tensor("aggr_sums", (AGGR_ROWS, D), F32, kind="Internal").ap()

    with ExitStack() as ctx:
        def sb(name, shape, dt=F32):
            return ctx.enter_context(nc.sbuf_tensor(name, shape, dt))

        def pb(name):
            return ctx.enter_context(nc.psum_tensor(name, [P, J, P], F32))

        def sem(name):
            return ctx.enter_context(nc.semaphore(name))

        def ring_sems(name):
            return [sem(f"{name}{i}") for i in range(RING)]

        ident = sb("ident", [P, P])
        later = sb("later", [P, BLOCK])
        spare = sb("spare", [P, J])
        zeros = sb("zeros", [P, ZERO_W])
        g1_row = sb("g1_row", [P, J, D])
        g1e_row = sb("g1e_row", [P, J, D])
        b1_row = sb("b1_row", [P, J, D])
        bg2_row = sb("bg2_row", [P, J, D])
        bf2_row = sb("bf2_row", [P, J, D])
        eps_col = sb("eps_col", [P, 1])
        b1_col = sb("b1_col", [P, 1])
        b1e_col = sb("b1e_col", [P, 1])
        bg1_col = sb("bg1_col", [P, 1])
        bg1e_col = sb("bg1e_col", [P, 1])
        g2_col = sb("g2_col", [P, 1])
        b2_col = sb("b2_col", [P, 1])
        bf1_col = sb("bf1_col", [P, KF])
        wg1 = sb("wg1", [P, D])
        wg2 = sb("wg2", [P, D])
        wf1 = sb("wf1", [P, DF])
        wf2 = sb("wf2", [P, KF, D])
        minus_half = sb("minus_half", [P, 2 * J])

        e_x = sb("e_x", [P, RING, J, D])
        e_attr = sb("e_attr", [P, RING, J, D])
        e_cols = sb("e_cols", [P, RING, 2, J], I32)
        e_dst = sb("e_dst", [P, RING, BLOCK], I32)
        e_dstf = sb("e_dstf", [P, RING, J])
        e_toward = sb("e_toward", [P, RING, J])
        e_relu = sb("e_relu", [P, RING, J, D])
        e_scaled = sb("e_scaled", [P, RING, J, D])
        e_attrb = sb("e_attrb", [P, RING, J, D])
        e_sum = sb("e_sum", [P, RING, J, D])
        e_msg = sb("e_msg", [P, RING, J, D])
        e_match = sb("e_match", [P, 2, 2 * (J + 1) * P])
        e_count = sb("e_count", [P, RING, J])
        e_extra = sb("e_extra", [P, RING, J])
        e_index = sb("e_index", [P, RING, J], I32)
        e_merged = sb("e_merged", [P, RING, J, D])
        e_stat = sb("e_stat", [P, RING, 2, J, 6])
        e_mom = sb("e_mom", [P, RING, 2, J, 2])
        e_var = sb("e_var", [P, RING, 2, J])
        e_rstd = sb("e_rstd", [P, RING, 2, J])

        n_x = sb("n_x", [P, RING, J, D])
        n_aggr = sb("n_aggr", [P, RING, J, D])
        n_xb = sb("n_xb", [P, RING, J, D])
        n_relu = sb("n_relu", [P, RING, J, D])
        n_z = sb("n_z", [P, 2, J, D])
        n_zg = sb("n_zg", [P, 2, J, D])
        n_in = sb("n_in", [P, 2, J, D])
        n_h = sb("n_h", [P, 2, J, D])
        n_hb = sb("n_hb", [P, RING, J, D])
        n_inT = sb("n_inT", [P, J, P])
        n_gT = sb("n_gT", [P, J, P])
        n_x2 = sb("n_x2", [P, RING, J, D])
        n_x2b = sb("n_x2b", [P, 2, J, D])
        n_z2 = sb("n_z2", [P, 2, J, D])
        n_z2T = sb("n_z2T", [P, 2, J, P])
        n_act = sb("n_act", [P, KF, J, P])
        n_out = sb("n_out", [P, 2, J, D])
        n_stat = sb("n_stat", [P, RING, 2, J, 6])
        n_mom = sb("n_mom", [P, RING, 2, J, 2])
        n_var = sb("n_var", [P, RING, 2, J])
        n_rstd = sb("n_rstd", [P, RING, 2, J])
        n_stat2 = sb("n_stat2", [P, RING, J, 6])
        n_mom2 = sb("n_mom2", [P, RING, J, 2])
        n_var2 = sb("n_var2", [P, RING, J])
        n_rstd2 = sb("n_rstd2", [P, RING, J])

        p_in, p_g, p_gout, p_z2, p_out = (pb(f"p_{n}") for n in ("in", "g", "gout", "z2", "out"))
        p_f = [pb(f"p_f{i}") for i in range(3)]
        p_merged = [p_gout, p_out]

        s_param = sem("s_param")
        s_const = sem("s_const")
        s_eps = sem("s_eps")
        s_scaled_params = sem("s_scaled_params")
        s_b1g = sem("s_b1g")
        s_bias = sem("s_bias")
        s_zeros = sem("s_zeros")
        s_zeroed = sem("s_zeroed")
        q_attr, q_cols, q_dst, q_gather, q_scatter = (
            ring_sems(n) for n in ("q_attr", "q_cols", "q_dst", "q_gather", "q_scatter"))
        s_ecopy, s_estat, s_emom, s_erelu, s_estatu, s_emomu, s_evar0, s_evar = (
            sem(n) for n in ("s_ecopy", "s_estat", "s_emom", "s_erelu", "s_estatu", "s_emomu",
                             "s_evar0", "s_evar"))
        s_erstd, s_escaled, s_eattrb, s_esum, s_emsg, s_ematch, s_eextra, s_eindex = (
            sem(n) for n in ("s_erstd", "s_escaled", "s_eattrb", "s_esum", "s_emsg", "s_ematch",
                             "s_eextra", "s_eindex"))
        s_emm, s_emerged = sem("s_emm"), sem("s_emerged")
        q_x, q_aggr, q_out = (ring_sems(n) for n in ("q_x", "q_aggr", "q_out"))
        s_nstat, s_nmom, s_nrelu, s_nstatu, s_nmomu, s_nvar0, s_nvar, s_nrstd, s_nz = (
            sem(n) for n in ("s_nstat", "s_nmom", "s_nrelu", "s_nstatu", "s_nmomu", "s_nvar0",
                             "s_nvar", "s_nrstd", "s_nz"))
        s_nxb, s_nzg, s_nh, s_nin, s_nhb, s_nx2b = (
            sem(n) for n in ("s_nxb", "s_nzg", "s_nh", "s_nin", "s_nhb", "s_nx2b"))
        s_tin, s_inT, s_g, s_gT, s_gout, s_x2, s_stat2, s_mom2, s_var2, s_rstd2, s_z2 = (
            sem(n) for n in ("s_tin", "s_inT", "s_g", "s_gT", "s_gout", "s_x2", "s_stat2",
                             "s_mom2", "s_var2", "s_rstd2", "s_z2"))
        s_tz2, s_z2T, s_f, s_act, s_fout, s_nout = (
            sem(n) for n in ("s_tz2", "s_z2T", "s_f", "s_act", "s_fout", "s_nout"))

        def rows_of(dram, item):
            start = item.at * BLOCK
            return dram[bass.ds(start, item.rows * J), :].rearrange("(p j) d -> p j d", j=J)

        def row(vector):
            return vector.unsqueeze(0).unsqueeze(0).to_broadcast([P, J, D])

        PARAMS = [
            (g1_row[:], row(g1)), (b1_row[:], row(b1)), (bg2_row[:], row(bg2)), (bf2_row[:], row(bf2)),
            (eps_col[:], eps_gin.unsqueeze(0).to_broadcast([P, 1])),
            (b1_col[:], b1.unsqueeze(1)), (bg1_col[:], bg1.unsqueeze(1)),
            (g2_col[:], g2.unsqueeze(1)), (b2_col[:], b2.unsqueeze(1)),
            (bf1_col[:], bf1.rearrange("(k p) -> p k", p=P)),
            (wg1[:], Wg1), (wg2[:], Wg2), (wf1[:], Wf1),
            (wf2[:], Wf2.rearrange("(k p) d -> p k d", p=P)),
        ]
        ALL_PARAMS = 16 * len(PARAMS)
        flat = aggr.rearrange("(p r) d -> p (r d)", p=P)
        ZW = flat.shape[1]
        ZREP = 8
        ZPARTS = [(a, min(ZREP, ZW // ZERO_W - a)) for a in range(0, ZW // ZERO_W, ZREP)]
        MATCH_AT = [sum(J - i for i in range(a)) * P for a in range(J)]

        block = ctx.enter_context(nc.Block())

        @block.sync
        def _(sp):
            def edge_loads(item_of):
                c = item_of(0)
                if c is None:
                    return
                reached(sp, s_ematch, c.at - RING + 1)
                reached(sp, s_eindex, c.at - RING + 1)
                reached(sp, q_gather[c.slot], c.turn * 16 * J)
                sp.dma_start(e_cols[0:c.rows, c.slot].rearrange("p a j -> p (a j)"),
                             edge_cols[bass.ds(c.at * P, c.rows), :]).then_inc(q_cols[c.slot], 16)
                sp.dma_start(e_dst[:, c.slot, :],
                             dst_rows[bass.ds(c.at, 1), :].to_broadcast([P, BLOCK])).then_inc(q_dst[c.slot], 16)
                reached(sp, s_eattrb, c.at - RING + 1)
                sp.dma_start(e_attr[0:c.rows, c.slot], rows_of(edge_attr, c)).then_inc(q_attr[c.slot], 16)

            with nc.allow_non_contiguous_dma(reason="vectors as columns"):
                for to, frm in PARAMS:
                    sp.dma_start(to, frm).then_inc(s_param, 16)
            pipeline(sp, NC, NC_TAIL, 0, edge_loads)

            def node_traffic(item_of):
                if (b := item_of(0)) is not None:
                    reached(sp, s_nrelu, b.at - RING + 1)
                    reached(sp, s_nxb, b.at - RING + 1)
                    sp.dma_start(n_x[0:b.rows, b.slot], rows_of(x, b)).then_inc(q_x[b.slot], 16)
                if (b := item_of(1)) is not None:
                    if isinstance(b.at, int) and b.at == 0:
                        for q in range(RING):
                            sp.wait_ge(q_scatter[q], 16 * J * len(range(q, NC, RING)))
                    reached(sp, s_nin, b.at - RING + 1)
                    sp.dma_start(n_aggr[0:b.rows, b.slot], rows_of(aggr, b)).then_inc(q_aggr[b.slot], 16)
                if (b := item_of(6)) is not None:
                    sp.wait_ge(s_nout, b.at + 1)
                    sp.dma_start(rows_of(out, b), n_out[0:b.rows, b.slot % 2]).then_inc(q_out[b.slot], 16)

            pipeline(sp, NB, NB_TAIL, 6, node_traffic)
            for q in range(RING):
                sp.wait_ge(q_out[q], 16 * len(range(q, NB, RING)))

        @block.gpsimd
        def _(pool):
            nc.gpsimd.memset(ident[:], 0.0).then_inc(s_const, 1)
            nc.gpsimd.memset(later[:], 1.0).then_inc(s_const, 1)
            nc.gpsimd.memset(minus_half[:], -0.5).then_inc(s_const, 1)
            nc.gpsimd.iota(spare[:], [[P, J]], base=N, channel_multiplier=1,
                           allow_small_or_imprecise_dtypes=True).then_inc(s_const, 1)
            pool.wait_ge(s_const, 4)
            nc.gpsimd.affine_select(out=ident[:], in_=ident[:], compare_op=ALU.not_equal, fill=1.0,
                                    base=0, pattern=[[-1, P]], channel_multiplier=1).then_inc(s_const, 1)
            nc.gpsimd.affine_select(out=later[:, 0:P], in_=later[:, 0:P], compare_op=ALU.is_ge, fill=0.0,
                                    base=0, pattern=[[1, P]], channel_multiplier=-1).then_inc(s_const, 1)

            def inverse_deviation(to, of, width):
                return nc.gpsimd.tensor_tensor(to, of, minus_half[0:to.shape[0], 0:width].rearrange(
                    "p (a j) -> p a j", j=J) if width == 2 * J else minus_half[0:to.shape[0], 0:width], ALU.pow)

            last_node, last_sum, bound = (pool.alloc_register(n) for n in ("last_node", "last_sum", "bound"))
            pool.reg_mov(last_node, N - 2)
            pool.reg_mov(last_sum, AGGR_ROWS - 2)

            def edges(item_of):
                if (c := item_of(0)) is not None:
                    pool.wait_ge(q_cols[c.slot], 16 * (c.turn + 1))
                    reached(pool, s_erelu, c.at - RING + 1)
                    pool.reg_add(bound, last_node, 1)
                    for j in range(J):
                        nc.gpsimd.indirect_dma_start(
                            out=e_x[0:c.rows, c.slot, j, :], out_offset=None, in_=x,
                            in_offset=bass.IndirectOffsetOnAxis(ap=e_cols[0:c.rows, c.slot, 0, j:j + 1], axis=0),
                            bounds_check=bound,
                        ).then_inc(q_gather[c.slot], 16)
                if (c := item_of(1)) is not None:
                    if isinstance(c.at, int) and c.at == 0:
                        pool.wait_ge(s_param, ALL_PARAMS)
                    pool.wait_ge(q_attr[c.slot], 16 * (c.turn + 1))
                    reached(pool, s_esum, c.at - RING + 1)
                    nc.gpsimd.tensor_tensor(e_attrb[0:c.rows, c.slot], e_attr[0:c.rows, c.slot],
                                            b1_row[0:c.rows], ALU.add).then_inc(s_eattrb, 1)
                    pool.wait_ge(s_evar, c.at + 1)
                    inverse_deviation(e_rstd[0:c.rows, c.slot], e_var[0:c.rows, c.slot], 2 * J).then_inc(s_erstd, 1)
                if (c := item_of(3)) is not None:
                    if isinstance(c.at, int) and c.at == 0:
                        pool.wait_ge(s_zeroed, 16 * len(ZPARTS))
                    pool.wait_ge(s_emerged, c.at + 1)
                    pool.wait_ge(s_eindex, c.at + 1)
                    if not (isinstance(c.at, int) and c.at == 0):
                        before = (c.slot - 1) % RING
                        pool.wait_ge(q_scatter[before], 16 * J * (c.turn + 1 if c.slot else c.turn))
                    pool.reg_add(bound, last_sum, 1)
                    for j in range(J):
                        nc.gpsimd.indirect_dma_start(
                            out=aggr, out_offset=bass.IndirectOffsetOnAxis(
                                ap=e_index[0:c.rows, c.slot, j:j + 1], axis=0),
                            in_=e_merged[0:c.rows, c.slot, j, :], in_offset=None,
                            bounds_check=bound, compute_op=ALU.add,
                        ).then_inc(q_scatter[c.slot], 16)

            pipeline(pool, NC, NC_TAIL, 3, edges)

            def nodes(item_of):
                if (b := item_of(3)) is not None:
                    pool.wait_ge(s_var2, b.at + 1)
                    inverse_deviation(n_rstd2[0:b.rows, b.slot], n_var2[0:b.rows, b.slot], J).then_inc(s_rstd2, 1)
                    reached(pool, s_nout, b.at - 1)
                    nc.gpsimd.tensor_tensor(n_x2b[0:b.rows, b.slot % 2], n_x2[0:b.rows, b.slot],
                                            n_xb[0:b.rows, b.slot], ALU.add).then_inc(s_nx2b, 1)
                if (b := item_of(0)) is not None:
                    pool.wait_ge(q_x[b.slot], 16 * (b.turn + 1))
                    nc.gpsimd.tensor_tensor(n_xb[0:b.rows, b.slot], n_x[0:b.rows, b.slot],
                                            bf2_row[0:b.rows], ALU.add).then_inc(s_nxb, 1)
                    pool.wait_ge(s_nvar, b.at + 1)
                    inverse_deviation(n_rstd[0:b.rows, b.slot], n_var[0:b.rows, b.slot], 2 * J).then_inc(s_nrstd, 1)
                    pool.wait_ge(s_nrstd, b.at + 1)
                    nc.gpsimd.tensor_tensor(
                        n_h[0:b.rows, b.slot % 2], n_relu[0:b.rows, b.slot],
                        n_rstd[0:b.rows, b.slot, 0, :].unsqueeze(2).to_broadcast([b.rows, J, D]),
                        ALU.mult).then_inc(s_nh, 1)
                if (b := item_of(1)) is not None:
                    pool.wait_ge(s_nz, b.at + 1)
                    nc.gpsimd.tensor_tensor(n_zg[0:b.rows, b.slot % 2], n_z[0:b.rows, b.slot % 2],
                                            g1e_row[0:b.rows], ALU.mult).then_inc(s_nzg, 1)
                    pool.wait_ge(s_nh, b.at + 1)
                    reached(pool, s_x2, b.at - RING + 1)
                    nc.gpsimd.tensor_tensor(n_hb[0:b.rows, b.slot], n_h[0:b.rows, b.slot % 2],
                                            bg2_row[0:b.rows], ALU.add).then_inc(s_nhb, 1)
                    pool.wait_ge(s_nzg, b.at + 1)
                    pool.wait_ge(q_aggr[b.slot], 16 * (b.turn + 1))
                    reached(pool, s_tin, b.at - 1)
                    nc.gpsimd.tensor_tensor(n_in[0:b.rows, b.slot % 2], n_zg[0:b.rows, b.slot % 2],
                                            n_aggr[0:b.rows, b.slot], ALU.add).then_inc(s_nin, 1)

            pool.wait_ge(s_scaled_params, 3)
            pipeline(pool, NB, NB_TAIL, 3, nodes)

        @block.scalar
        def _(act):
            act.wait_ge(s_zeros, 1)
            for a, w in ZPARTS:
                act.dma_start(flat[:, a * ZERO_W:(a + w) * ZERO_W].rearrange("p (a w) -> p a w", w=ZERO_W),
                              zeros[:].unsqueeze(1).to_broadcast([P, w, ZERO_W])).then_inc(s_zeroed, 16)

            def edges(item_of):
                if (c := item_of(3)) is not None:
                    act.wait_ge(s_emm, c.at + 1)
                    if not isinstance(c.turn, int) or c.turn > 0:
                        act.wait_ge(q_scatter[c.slot], 16 * J * c.turn)
                    nc.scalar.activation(e_merged[0:c.rows, c.slot], p_merged[c.slot % 2][0:c.rows],
                                         ACT.Identity).then_inc(s_emerged, 1)
                if (c := item_of(2)) is not None:
                    act.wait_ge(s_esum, c.at + 1)
                    reached(act, s_emm, c.at - RING + 1)
                    nc.scalar.activation(e_msg[0:c.rows, c.slot], e_sum[0:c.rows, c.slot],
                                         ACT.Relu).then_inc(s_emsg, 1)

            pipeline(act, NC, NC_TAIL, 3, edges)

            def nodes(item_of):
                if (b := item_of(2)) is not None:
                    act.wait_ge(s_tin, b.at + 1)
                    reached(act, s_g, b.at)
                    nc.scalar.activation(n_inT[:, :, 0:b.rows], p_in[:, :, 0:b.rows],
                                         ACT.Identity).then_inc(s_inT, 1)
                if (b := item_of(4)) is not None:
                    reached(act, s_fout, b.at)
                    for k in range(KF):
                        act.wait_ge(s_f, b.at * KF + (k + 1))
                        nc.scalar.activation(n_act[:, k, :, 0:b.rows], p_f[k % 3][:, :, 0:b.rows],
                                             ACT.Gelu, bias=bf1_col[:, k:k + 1]).then_inc(s_act, 1)
                if (b := item_of(2)) is not None:
                    if isinstance(b.at, int) and b.at == 0:
                        act.wait_ge(s_bias, 1)
                    act.wait_ge(s_g, b.at + 1)
                    reached(act, s_gout, b.at)
                    nc.scalar.activation(n_gT[:, :, 0:b.rows], p_g[:, :, 0:b.rows], ACT.Relu,
                                         bias=bg1e_col[:, 0:1]).then_inc(s_gT, 1)
                if (b := item_of(3)) is not None:
                    act.wait_ge(s_tz2, b.at + 1)
                    reached(act, s_f, (b.at - 1) * KF)
                    nc.scalar.activation(n_z2T[:, b.slot % 2, :, 0:b.rows], p_z2[:, :, 0:b.rows], ACT.Identity,
                                         bias=b2_col[:, 0:1], scale=g2_col[:, 0:1]).then_inc(s_z2T, 1)

            pipeline(act, NB, NB_TAIL, 4, nodes)

        @block.vector
        def _(dve):
            nc.vector.memset(zeros[:], 0.0).then_inc(s_zeros, 1)
            dve.wait_ge(s_param, ALL_PARAMS)
            nc.vector.tensor_scalar(eps_col[:], eps_col[:], 1.0, None, ALU.add).then_inc(s_eps, 1)
            dve.wait_ge(s_eps, 1)
            nc.vector.tensor_scalar(b1e_col[:], b1_col[:], eps_col[:, 0:1], None, ALU.mult).then_inc(s_scaled_params, 1)
            nc.vector.tensor_scalar(g1e_row[:], g1_row[:], eps_col[:, 0:1], None, ALU.mult).then_inc(s_scaled_params, 1)
            dve.wait_ge(s_b1g, 1)
            nc.vector.tensor_tensor(bg1e_col[:], p_g[:, 0, 0:1], bg1_col[:], ALU.add).then_inc(s_bias, 1)
            dve.wait_ge(s_const, 6)
            nc.vector.memset(e_extra[:], 0.0).then_inc(s_scaled_params, 1)

            def stats(to, of, rows, done):
                for j in range(J):
                    last = nc.vector.bn_stats(to[0:rows, j, :], of[0:rows, j, :])
                last.then_inc(done, 1)

            def moments(to, of, rows, done):
                for j in range(J):
                    last = nc.vector.bn_aggr(to[0:rows, j, :], of[0:rows, j, :])
                last.then_inc(done, 1)

            def centred_relu(to, of, mom, rows, done):
                for j in range(J):
                    last = nc.vector.tensor_scalar(to[0:rows, j, :], of[0:rows, j, :], mom[0:rows, j, 0:1],
                                                   0.0, ALU.subtract, ALU.max)
                last.then_inc(done, 1)

            def both_variances(var, mom, rows, between, at, done):
                nc.vector.tensor_scalar(var[0:rows, 0, :], mom[0:rows, 0, :, 1], EPS, None,
                                        ALU.add).then_inc(between, 1)
                dve.wait_ge(between, at + 1)
                nc.vector.scalar_tensor_tensor(var[0:rows, 1, :], var[0:rows, 0, :], EPS,
                                               mom[0:rows, 1, :, 1], ALU.mult, ALU.add).then_inc(done, 1)

            def edges(item_of):
                if (c := item_of(1)) is not None:
                    s, r = c.slot, c.rows
                    dve.wait_ge(q_gather[s], 16 * J * (c.turn + 1))
                    stats(e_stat[:, s, 0], e_x[:, s], r, s_estat)
                    reached(dve, s_eindex, c.at - RING + 1)
                    dve.wait_ge(s_estat, c.at + 1)
                    nc.vector.tensor_copy(e_dstf[0:r, s], e_cols[0:r, s, 1, :]).then_inc(s_ecopy, 1)
                    moments(e_mom[:, s, 0], e_stat[:, s, 0], r, s_emom)
                    dve.wait_ge(s_ecopy, 2 * c.at + 1)
                    nc.vector.tensor_tensor(e_toward[0:r, s], spare[0:r], e_dstf[0:r, s],
                                            ALU.subtract).then_inc(s_ecopy, 1)
                    dve.wait_ge(s_emom, c.at + 1)
                    centred_relu(e_relu[:, s], e_x[:, s], e_mom[:, s, 0], r, s_erelu)
                    dve.wait_ge(q_dst[s], 16 * (c.turn + 1))
                    reached(dve, s_emm, c.at - 1)
                    for a in range(J):
                        w = (J - a) * P
                        last = nc.vector.scalar_tensor_tensor(
                            e_match[0:r, s % 2, MATCH_AT[a]:MATCH_AT[a] + w], e_dst[0:r, s, a * P:BLOCK],
                            e_dstf[0:r, s, a:a + 1], later[0:r, 0:w], ALU.is_equal, ALU.mult,
                            accum_out=e_count[0:r, s, a:a + 1])
                        if a == 0:
                            dve.wait_ge(s_erelu, c.at + 1)
                    last.then_inc(s_ematch, 1)
                    stats(e_stat[:, s, 1], e_relu[:, s], r, s_estatu)
                    dve.wait_ge(s_ematch, c.at + 1)
                    dve.wait_ge(s_estatu, c.at + 1)
                    nc.vector.scalar_tensor_tensor(e_extra[0:r, s], e_count[0:r, s], 1.5, e_toward[0:r, s],
                                                   ALU.is_gt, ALU.mult).then_inc(s_eextra, 1)
                    moments(e_mom[:, s, 1], e_stat[:, s, 1], r, s_emomu)
                    if not isinstance(c.turn, int) or c.turn > 0:
                        dve.wait_ge(q_scatter[s], 16 * J * c.turn)
                    dve.wait_ge(s_eextra, c.at + 1)
                    nc.vector.tensor_tensor(e_index[0:r, s], e_dstf[0:r, s], e_extra[0:r, s],
                                            ALU.add).then_inc(s_eindex, 1)
                    dve.wait_ge(s_emomu, c.at + 1)
                    both_variances(e_var[:, s], e_mom[:, s], r, s_evar0, c.at, s_evar)
                    for j in range(J):
                        last = nc.vector.scalar_tensor_tensor(
                            e_scaled[0:r, s, j, :], e_relu[0:r, s, j, :], e_mom[0:r, s, 1, j, 0:1],
                            g1_row[0:r, j, :], ALU.subtract, ALU.mult)
                    last.then_inc(s_escaled, 1)
                if (c := item_of(2)) is not None:
                    s, r = c.slot, c.rows
                    dve.wait_ge(s_escaled, c.at + 1)
                    dve.wait_ge(s_erstd, c.at + 1)
                    dve.wait_ge(s_eattrb, c.at + 1)
                    reached(dve, s_emsg, c.at - RING + 1)
                    for j in range(J):
                        last = nc.vector.scalar_tensor_tensor(
                            e_sum[0:r, s, j, :], e_scaled[0:r, s, j, :], e_rstd[0:r, s, 1, j:j + 1],
                            e_attrb[0:r, s, j, :], ALU.mult, ALU.add)
                    last.then_inc(s_esum, 1)

            pipeline(dve, NC, NC_TAIL, 2, edges)

            def nodes(item_of):
                first, second, third, fourth = item_of(0), item_of(1), item_of(3), item_of(4)
                if (b := third) is not None:
                    dve.wait_ge(s_gout, b.at + 1)
                    dve.wait_ge(s_nhb, b.at + 1)
                    reached(dve, s_nx2b, b.at - RING + 1)
                    nc.vector.tensor_tensor(n_x2[0:b.rows, b.slot], p_gout[0:b.rows], n_hb[0:b.rows, b.slot],
                                            ALU.add).then_inc(s_x2, 1)
                if (b := first) is not None:
                    dve.wait_ge(q_x[b.slot], 16 * (b.turn + 1))
                    stats(n_stat[:, b.slot, 0], n_x[:, b.slot], b.rows, s_nstat)
                if (b := first) is not None:
                    dve.wait_ge(s_nstat, b.at + 1)
                if (b := third) is not None:
                    dve.wait_ge(s_x2, b.at + 1)
                    stats(n_stat2[:, b.slot], n_x2[:, b.slot], b.rows, s_stat2)
                if (b := first) is not None:
                    moments(n_mom[:, b.slot, 0], n_stat[:, b.slot, 0], b.rows, s_nmom)
                if (b := third) is not None:
                    dve.wait_ge(s_stat2, b.at + 1)
                if (b := second) is not None:
                    dve.wait_ge(s_nrstd, b.at + 1)
                    reached(dve, s_nzg, b.at - 1)
                    for j in range(J):
                        last = nc.vector.tensor_scalar(
                            n_z[0:b.rows, b.slot % 2, j, :], n_relu[0:b.rows, b.slot, j, :],
                            n_mom[0:b.rows, b.slot, 1, j, 0:1], n_rstd[0:b.rows, b.slot, 1, j:j + 1],
                            ALU.subtract, ALU.mult)
                    last.then_inc(s_nz, 1)
                if (b := third) is not None:
                    moments(n_mom2[:, b.slot], n_stat2[:, b.slot], b.rows, s_mom2)
                if (b := first) is not None:
                    dve.wait_ge(s_nmom, b.at + 1)
                    reached(dve, s_nh, b.at - RING + 1)
                    centred_relu(n_relu[:, b.slot], n_x[:, b.slot], n_mom[:, b.slot, 0], b.rows, s_nrelu)
                if (b := third) is not None:
                    dve.wait_ge(s_mom2, b.at + 1)
                    nc.vector.tensor_scalar(n_var2[0:b.rows, b.slot], n_mom2[0:b.rows, b.slot, :, 1], EPS, None,
                                            ALU.add).then_inc(s_var2, 1)
                if (b := first) is not None:
                    dve.wait_ge(s_nrelu, b.at + 1)
                    stats(n_stat[:, b.slot, 1], n_relu[:, b.slot], b.rows, s_nstatu)
                    dve.wait_ge(s_nstatu, b.at + 1)
                if (b := third) is not None:
                    dve.wait_ge(s_rstd2, b.at + 1)
                    reached(dve, s_tz2, b.at - 1)
                    for j in range(J):
                        last = nc.vector.tensor_scalar(
                            n_z2[0:b.rows, b.slot % 2, j, :], n_x2[0:b.rows, b.slot, j, :],
                            n_mom2[0:b.rows, b.slot, j, 0:1], n_rstd2[0:b.rows, b.slot, j:j + 1],
                            ALU.subtract, ALU.mult)
                    last.then_inc(s_z2, 1)
                if (b := first) is not None:
                    moments(n_mom[:, b.slot, 1], n_stat[:, b.slot, 1], b.rows, s_nmomu)
                    dve.wait_ge(s_nmomu, b.at + 1)
                    both_variances(n_var[:, b.slot], n_mom[:, b.slot], b.rows, s_nvar0, b.at, s_nvar)
                if (b := fourth) is not None:
                    dve.wait_ge(s_fout, b.at + 1)
                    dve.wait_ge(s_nx2b, b.at + 1)
                    free = b.slot - 2
                    if isinstance(b.at, int):
                        reached(dve, q_out[free % RING], 16 * ((b.at - 2) // RING + 1))
                    else:
                        dve.wait_ge(q_out[free % RING], 16 * (b.turn + 1 if free >= 0 else b.turn))
                    nc.vector.tensor_tensor(n_out[0:b.rows, b.slot % 2], p_out[0:b.rows],
                                            n_x2b[0:b.rows, b.slot % 2], ALU.add).then_inc(s_nout, 1)

            pipeline(dve, NB, NB_TAIL, 4, nodes)

        @block.tensor
        def _(pe):
            pe.wait_ge(s_scaled_params, 1)
            nc.tensor.matmul(p_g[:, 0, 0:1], wg1[:], b1e_col[:], start=True, stop=True).then_inc(s_b1g, 1)

            def edges(item_of):
                if (c := item_of(2)) is not None:
                    s, r = c.slot, c.rows
                    pe.wait_ge(s_ematch, c.at + 1)
                    pe.wait_ge(s_emsg, c.at + 1)
                    reached(pe, s_emerged, c.at - 1)
                    for i in range(J):
                        for a in range(i + 1):
                            m = MATCH_AT[a] + (i - a) * P
                            last = nc.tensor.matmul(p_merged[s % 2][0:r, i, :], e_match[0:r, s % 2, m:m + r],
                                                    e_msg[0:r, s, a, :], start=(a == 0), stop=(a == i))
                    last.then_inc(s_emm, 1)

            pipeline(pe, NC, NC_TAIL, 2, edges)

            def nodes(item_of):
                second, third, fourth = item_of(2), item_of(3), item_of(4)
                if (b := second) is not None:
                    if isinstance(b.at, int) and b.at == 0:
                        pe.wait_ge(s_emerged, NC)
                        pe.wait_ge(s_const, 6)
                        pe.wait_ge(s_bias, 1)
                    pe.wait_ge(s_nin, b.at + 1)
                    reached(pe, s_inT, b.at)
                    for j in range(J):
                        last = nc.tensor.transpose(p_in[:, j, 0:b.rows], n_in[0:b.rows, b.slot % 2, j, :],
                                                   ident[0:b.rows, 0:b.rows])
                    last.then_inc(s_tin, 1)
                if (b := fourth) is not None:
                    pe.wait_ge(s_z2T, b.at + 1)
                    for k in range(KF):
                        reached(pe, s_act, b.at * KF + k - 2)
                        nc.tensor.matmul(p_f[k % 3][:, :, 0:b.rows], wf1[:, k * P:(k + 1) * P],
                                         n_z2T[:, b.slot % 2, :, 0:b.rows], start=True, stop=True).then_inc(s_f, 1)
                if (b := second) is not None:
                    pe.wait_ge(s_inT, b.at + 1)
                    reached(pe, s_gT, b.at)
                    nc.tensor.matmul(p_g[:, :, 0:b.rows], wg1[:], n_inT[:, :, 0:b.rows],
                                     start=True, stop=True).then_inc(s_g, 1)
                if (b := fourth) is not None:
                    reached(pe, s_nout, b.at)
                    for k in range(KF):
                        pe.wait_ge(s_act, b.at * KF + (k + 1))
                        for j in range(J):
                            last = nc.tensor.matmul(p_out[0:b.rows, j, :], n_act[:, k, j, 0:b.rows], wf2[:, k, :],
                                                    start=(k == 0 and j == 0), stop=(k == KF - 1),
                                                    skip_group_check=True)
                    last.then_inc(s_fout, 1)
                if (b := second) is not None:
                    pe.wait_ge(s_gT, b.at + 1)
                    reached(pe, s_x2, b.at)
                    for j in range(J):
                        last = nc.tensor.matmul(p_gout[0:b.rows, j, :], n_gT[:, j, 0:b.rows], wg2[:],
                                                start=True, stop=True)
                    last.then_inc(s_gout, 1)
                if (b := third) is not None:
                    pe.wait_ge(s_z2, b.at + 1)
                    reached(pe, s_z2T, b.at)
                    for j in range(J):
                        last = nc.tensor.transpose(p_z2[:, j, 0:b.rows], n_z2[0:b.rows, b.slot % 2, j, :],
                                                   ident[0:b.rows, 0:b.rows])
                    last.then_inc(s_tz2, 1)

            pipeline(pe, NB, NB_TAIL, 4, nodes)


_WEIGHTS = ["g1", "b1", "g2", "b2", "eps_gin", "Wg1", "bg1", "Wg2", "bg2", "Wf1", "bf1", "Wf2", "bf2"]


def kernel(**inputs):
    import numpy as _np
    import concourse.bacc as _bacc
    from concourse import mybir as _mybir
    from concourse.bass_utils import run_bass_kernel_spmd as _run

    x = _np.ascontiguousarray(inputs["x"])
    attr = _np.ascontiguousarray(inputs["edge_attr_128"])
    chunks = -(-attr.shape[0] // BLOCK)
    pad = chunks * BLOCK - attr.shape[0]
    src = _np.pad(_np.asarray(inputs["src"]), (0, pad)).reshape(chunks, P, 1, J)
    dst = _np.pad(_np.asarray(inputs["dst"]), (0, pad), constant_values=-1).reshape(chunks, P, 1, J)
    arrays = {"in_x": x, "in_attr": attr,
              "in_edge_cols": _np.ascontiguousarray(_np.concatenate([src, dst], 2).reshape(chunks * P, 2 * J)),
              "in_dst_rows": _np.ascontiguousarray(dst[:, :, 0].transpose(0, 2, 1).reshape(chunks, BLOCK))}
    for name in _WEIGHTS:
        arrays[f"in_{name}"] = _np.ascontiguousarray(inputs[f"L0_gnn_{name}"])
    arrays["in_eps_gin"] = arrays["in_eps_gin"].reshape(1)

    nc = _bacc.Bacc("TRN2", target_bir_lowering=False, num_devices=1)
    args = [nc.dram_tensor(n, a.shape, _mybir.dt.from_np(a.dtype), kind="ExternalInput").ap()
            for n, a in arrays.items()]
    out = nc.dram_tensor("out_dram", x.shape, _mybir.dt.float32, kind="ExternalOutput").ap()
    gnn_kernel(nc, *args, out)
    r = _run(nc, [arrays], core_ids=[0])
    return r.results[0]["out_dram"]
```

```python
from contextlib import ExitStack

import concourse.bass as bass
from concourse import mybir

ALU = mybir.AluOpType
ACT = mybir.ActivationFunctionType
F32 = mybir.dt.float32
I32 = mybir.dt.int32

BF16 = mybir.dt.bfloat16

P = 128
J = 4
BLOCK = P * J
NODE_TURN = 6
EDGE_TURN = 3
EPS = 1e-5

EDGE_LAG = 3
NODE_LAG = 7
SP_LAG = 9
SUMS_AT = 2
LEAD = 4


class Item:

    def __init__(self, value, unroll, k, rows):
        self.value, self.unroll, self.k, self.rows = value, unroll, k, rows
        self.at = value * unroll + k
        self.fixed = isinstance(value, int)

    def slot(self, depth):
        return self.k % depth

    def uses(self, depth):
        return self.value * (self.unroll // depth) + self.k // depth

    def is_number(self, n):
        return self.fixed and self.k == n


class Work:

    def __init__(self, count, tail_rows, unroll):
        self.count, self.tail_rows, self.unroll = count, tail_rows, unroll

    def at_step(self, t):
        def item_of(o):
            if t - o < 0 or t - o >= self.count:
                return None
            return Item(0, self.unroll, t - o, self.tail_rows if t - o == self.count - 1 else P)
        return item_of

    def in_loop(self, n, k):
        return lambda o: Item(n, self.unroll, k - o, P)


def nothing(o):
    return None


def edges_then_nodes(eng, edges, nodes, edge_lag, node_lag, step):
    first, last = 2, (edges.count - 1) // EDGE_TURN
    for t in range(first * EDGE_TURN):
        step(nothing, edges.at_step(t), (0, 1), True)
    with eng.Fori(first, last) as n:
        for k in range(EDGE_TURN):
            step(nothing, edges.in_loop(n, k), (0, 1), True)
    for t in range(last * EDGE_TURN, edges.count + edge_lag):
        step(nothing, edges.at_step(t), (0, 1), True)
    first, last = 2, (nodes.count - 1) // NODE_TURN
    for t in range(first * NODE_TURN):
        step(nodes.at_step(t), nothing, (), True)
    with eng.Fori(first, last) as n:
        for k in range(NODE_TURN):
            step(nodes.in_loop(n, k), nothing, (), True)
    for t in range(last * NODE_TURN, nodes.count + node_lag):
        step(nodes.at_step(t), nothing, (), True)


def edges_beside_nodes(eng, edges, nodes, edge_lag, node_lag, step):
    def peeled(t):
        step(nodes.at_step(t), edges.at_step(LEAD + t // 2), (t % 2,), False)

    for t in range(LEAD):
        step(nothing, edges.at_step(t), (0, 1), False)
    first = 2
    last = 2 * (edges.count - 1 - LEAD) // NODE_TURN
    for t in range(first * NODE_TURN):
        peeled(t)
    with eng.Fori(first, last) as n:
        for k in range(NODE_TURN):
            step(nodes.in_loop(n, k), edges.in_loop(n, LEAD + k // 2), (k % 2,), False)
    for t in range(last * NODE_TURN, nodes.count + node_lag):
        peeled(t)


def reached(eng, sem, value):
    if isinstance(value, int) and value <= 0:
        return
    eng.wait_ge(sem, value)


def gnn_kernel(nc, x, edge_attr, edge_cols, dst_rows, g1, b1, g2, b2, eps_gin,
               Wg1, bg1, Wg2, bg2, Wf1, bf1, Wf2, bf2, out):
    N, D = x.shape
    E = edge_attr.shape[0]
    DF = Wf1.shape[1]
    KF = DF // P
    NB, NC = -(-N // BLOCK), -(-E // BLOCK)
    NB_TAIL, NC_TAIL = (N - (NB - 1) * BLOCK) // J, (E - (NC - 1) * BLOCK) // J
    assert D == P and NB_TAIL * J + (NB - 1) * BLOCK == N and NC_TAIL * J + (NC - 1) * BLOCK == E
    NODES, EDGES = Work(NB, NB_TAIL, NODE_TURN), Work(NC, NC_TAIL, EDGE_TURN)

    ZERO_W = 1024
    ZERO_ROWS = 4096
    AGGR_ROWS = -(-(N + BLOCK) // ZERO_W) * ZERO_W
    aggr = nc.dram_tensor("aggr_sums", (AGGR_ROWS, D), F32, kind="Internal").ap()
    ZERO_PARTS = [(max(0, hi - ZERO_ROWS), hi) for hi in range(AGGR_ROWS, 0, -ZERO_ROWS)]

    with ExitStack() as ctx:
        def sb(name, shape, dt=F32):
            return ctx.enter_context(nc.sbuf_tensor(name, shape, dt))

        def pb(name):
            return ctx.enter_context(nc.psum_tensor(name, [P, J, P], F32))

        def sem(name):
            return ctx.enter_context(nc.semaphore(name))

        def ring_sems(name, depth):
            return [sem(f"{name}{i}") for i in range(depth)]

        ident = sb("ident", [P, P])
        later = sb("later", [P, BLOCK])
        spare = sb("spare", [P, J])
        zeros = sb("zeros", [P, ZERO_W])
        ones = sb("ones", [P, P], BF16)
        ones_col = sb("ones_col", [P, 1])
        minus_half = sb("minus_half", [P, 2 * J])
        g1_row = sb("g1_row", [P, J, D])
        g1e_row = sb("g1e_row", [P, J, D])
        b1_row = sb("b1_row", [P, J, D])
        bias_row = sb("bias_row", [P, 2, D])
        bias_rest = sb("bias_rest", [P, 2, D])
        bias_part = sb("bias_part", [P, 3, 2, D], BF16)
        bias_rows = sb("bias_rows", [P, 2, J, D], BF16)
        eps_col = sb("eps_col", [P, 1])
        b1_col = sb("b1_col", [P, 1])
        b1e_col = sb("b1e_col", [P, 1])
        bg1_col = sb("bg1_col", [P, 1])
        bg1e_col = sb("bg1e_col", [P, 1])
        g2_col = sb("g2_col", [P, 1])
        b2_col = sb("b2_col", [P, 1])
        bf1_col = sb("bf1_col", [P, KF])
        wg1 = sb("wg1", [P, D])
        wg2 = sb("wg2", [P, D])
        wf1 = sb("wf1", [P, DF])
        wf2 = sb("wf2", [P, KF, D])
        o_dst = sb("o_dst", [NC, BLOCK], I32)
        o_high, o_low, o_high_limit, o_low_limit, o_above, o_below, o_bad = (
            sb(f"o_{n}", [NC, 1]) for n in ("high", "low", "high_limit", "low_limit", "above", "below", "bad"))
        o_flag = sb("o_flag", [1, 1], I32)

        e_x, e_attr, e_relu, e_scaled, e_attrb, e_sum, e_msg, e_merged = (
            sb(f"e_{n}", [P, 3, J, D]) for n in ("x", "attr", "relu", "scaled", "attrb", "sum", "msg", "merged"))
        e_cols = sb("e_cols", [P, 3, 2, J], I32)
        e_dst = sb("e_dst", [P, 3, BLOCK], I32)
        e_dstf, e_toward, e_count, e_extra = (
            sb(f"e_{n}", [P, 3, J]) for n in ("dstf", "toward", "count", "extra"))
        e_match = sb("e_match", [P, 3, J * (J + 1) // 2 * P])
        e_index = sb("e_index", [P, 3, J], I32)
        e_stat = sb("e_stat", [P, 3, 2, J, 6])
        e_mom = sb("e_mom", [P, 3, 2, J, 2])
        e_var, e_rstd = (sb(f"e_{n}", [P, 3, 2, J]) for n in ("var", "rstd"))

        n_x, n_h, n_x2b = (sb(f"n_{n}", [P, 6, J, D]) for n in ("x", "h", "x2b"))
        n_aggr, n_relu, n_x2 = (sb(f"n_{n}", [P, 3, J, D]) for n in ("aggr", "relu", "x2"))
        n_z, n_zg, n_in, n_z2, n_out = (sb(f"n_{n}", [P, 2, J, D]) for n in ("z", "zg", "in", "z2", "out"))
        n_inT, n_gT, n_z2T = (sb(f"n_{n}", [P, 2, J, P]) for n in ("inT", "gT", "z2T"))
        n_act = sb("n_act", [P, KF, J, P])
        n_stat = sb("n_stat", [P, 6, 2, J, 6])
        n_mom = sb("n_mom", [P, 6, 2, J, 2])
        n_var, n_rstd = (sb(f"n_{n}", [P, 6, 2, J]) for n in ("var", "rstd"))
        n_stat2 = sb("n_stat2", [P, 6, J, 6])
        n_mom2 = sb("n_mom2", [P, 6, J, 2])
        n_shift, n_var2, n_rstd2, n_shift2 = (
            sb(f"n_{n}", [P, 6, J]) for n in ("shift", "var2", "rstd2", "shift2"))

        p_in, p_g, p_gout, p_z2, p_out, p_merged = (
            pb(f"p_{n}") for n in ("in", "g", "gout", "z2", "out", "merged"))
        p_f = [pb(f"p_f{i}") for i in range(2)]

        (s_param, s_const, s_ones, s_eps, s_scaled_params, s_b1g, s_bias, s_zeros, s_part, s_rows,
         s_order_in, s_bounds, s_order, s_bad, s_flag) = (sem(f"s_{n}") for n in (
             "param", "const", "ones", "eps", "scaled_params", "b1g", "bias", "zeros", "part", "rows",
             "order_in", "bounds", "order", "bad", "flag"))
        s_zeroed = [sem(f"s_zeroed{i}") for i in range(len(ZERO_PARTS))]
        q_attr, q_cols, q_dst, q_gather, q_scatter = (
            ring_sems(f"q_{n}", 3) for n in ("attr", "cols", "dst", "gather", "scatter"))
        (s_ecopy, s_etoward, s_estat, s_emom, s_erelu, s_estatu, s_emomu, s_evar0, s_evar, s_erstd,
         s_escaled, s_eattrb, s_esum, s_emsg, s_ematch, s_eextra, s_eindex, s_emm, s_emerged) = (
            sem(f"s_e{n}") for n in (
                "copy", "toward", "stat", "mom", "relu", "statu", "momu", "var0", "var", "rstd",
                "scaled", "attrb", "sum", "msg", "match", "extra", "index", "mm", "merged"))
        q_x, q_aggr, q_out = ring_sems("q_x", 6), ring_sems("q_aggr", 3), ring_sems("q_out", 2)
        (s_nstat, s_nmom, s_nrelu, s_nstatu, s_nmomu, s_nvar0, s_nvar, s_nrstd, s_nshift, s_nz, s_nh,
         s_nzg, s_nin, s_tin, s_inT, s_g, s_gT, s_gout, s_x2, s_stat2, s_mom2, s_var2, s_rstd2,
         s_shift2, s_x2b, s_z2, s_tz2, s_z2T, s_f, s_act, s_fout, s_nout) = (
            sem(f"s_n{n}") for n in (
                "stat", "mom", "relu", "statu", "momu", "var0", "var", "rstd", "shift", "z", "h",
                "zg", "in", "tin", "inT", "g", "gT", "gout", "x2", "stat2", "mom2", "var2", "rstd2",
                "shift2", "x2b", "z2", "tz2", "z2T", "f", "act", "fout", "out"))

        def rows_of(dram, item, work):
            if item.is_number(work.count - 1):
                start = 0
            else:
                start = item.value * (-item.unroll * BLOCK * D) + (dram.shape[0] - BLOCK * (item.k + 1)) * D
            return dram.rearrange("n d -> (n d)")[bass.ds(start, item.rows * J * D)].rearrange(
                "(p j d) -> p j d", j=J, d=D)

        def row(vector, times=None):
            if times is None:
                return vector.unsqueeze(0).to_broadcast([P, D])
            return vector.unsqueeze(0).unsqueeze(0).to_broadcast([P, times, D])

        PARAMS = [
            (g1_row[:], row(g1, J)), (b1_row[:], row(b1, J)), (bias_row[:, 0], row(bg2)), (bias_row[:, 1], row(bf2)),
            (eps_col[:], eps_gin.unsqueeze(0).to_broadcast([P, 1])),
            (b1_col[:], b1.unsqueeze(1)), (bg1_col[:], bg1.unsqueeze(1)),
            (g2_col[:], g2.unsqueeze(1)), (b2_col[:], b2.unsqueeze(1)),
            (bf1_col[:], bf1.rearrange("(k p) -> p k", p=P)),
            (wg1[:], Wg1), (wg2[:], Wg2), (wf1[:], Wf1),
            (wf2[:], Wf2.rearrange("(k p) d -> p k d", p=P)),
        ]
        ALL_PARAMS = 16 * len(PARAMS)
        SCATTERED = 16 * J
        MATCH_AT = [sum(J - i for i in range(a)) * P for a in range(J)]

        def branch(eng, edge_lag, node_lag, step):
            eng.wait_ge(s_flag, 1)
            unordered = eng.alloc_register("unordered")
            eng.reg_load(unordered, o_flag[0:1, 0:1])
            with eng.If_eq(unordered, 0):
                edges_beside_nodes(eng, EDGES, NODES, edge_lag, node_lag, step)
            with eng.Else():
                edges_then_nodes(eng, EDGES, NODES, edge_lag, node_lag, step)

        block = ctx.enter_context(nc.Block())

        @block.sync
        def _(sp):
            sp.dma_start(o_dst[:], dst_rows).then_inc(s_order_in, 16)
            with nc.allow_non_contiguous_dma(reason="vectors as columns"):
                for to, frm in PARAMS:
                    sp.dma_start(to, frm).then_inc(s_param, 16)

            count_registers = [sp.alloc_register(f"count{i}") for i in range(2)]

            def counts(item, *values):
                if item.fixed:
                    return values
                for register, v in zip(count_registers, values):
                    sp.reg_mov(register, v)
                sp.wait_ge(s_flag, 1)
                return count_registers[0:len(values)]

            def set_to_zero(parts):
                for part in parts:
                    lo, hi = ZERO_PARTS[part]
                    a = (hi - lo) * D // P // ZERO_W
                    sp.dma_start(aggr[lo:hi, :].rearrange("(p a r) d -> p a (r d)", p=P, a=a),
                                 zeros[:].unsqueeze(1).to_broadcast([P, a, ZERO_W])).then_inc(s_zeroed[part], 16)

            def step(node, edge, halves, apart):
                if apart and (c := edge(0)) is not None and c.is_number(0):
                    set_to_zero(range(len(ZERO_PARTS)))
                if not apart:
                    for item, ahead in ((edge(0), 0), (node(0), LEAD)):
                        if item is not None and item.fixed and item.k + ahead < len(ZERO_PARTS) and (
                                item.k < LEAD if item.unroll == EDGE_TURN else True):
                            set_to_zero([item.k + ahead])
                if 0 in halves and (c := edge(0)) is not None:
                    s = c.slot(3)
                    attributes = rows_of(edge_attr, c, EDGES)
                    cols = edge_cols.rearrange("n a -> (n a)")[bass.ds(
                        c.value * (c.unroll * BLOCK * 2) + c.k * BLOCK * 2,
                        c.rows * 2 * J)].rearrange("(p a) -> p a", p=c.rows)
                    destinations = dst_rows.rearrange("c i -> (c i)")[bass.ds(
                        c.value * (c.unroll * BLOCK) + c.k * BLOCK, BLOCK)]
                    before, gathered = counts(c, c.at - 2, c.uses(3) * 16 * J)
                    reached(sp, s_ematch, before)
                    reached(sp, s_eindex, before)
                    reached(sp, s_etoward, before)
                    reached(sp, q_gather[s], gathered)
                    sp.dma_start(e_cols[0:c.rows, s].rearrange("p a j -> p (a j)"), cols).then_inc(q_cols[s], 16)
                    sp.dma_start(e_dst[:, s, :], destinations.unsqueeze(0).to_broadcast([P, BLOCK])
                                 ).then_inc(q_dst[s], 16)
                    before, = counts(c, c.at - 2)
                    reached(sp, s_eattrb, before)
                    sp.dma_start(e_attr[0:c.rows, s], attributes).then_inc(q_attr[s], 16)
                if (b := node(0)) is not None:
                    rows = rows_of(x, b, NODES)
                    before, = counts(b, b.at - 5)
                    reached(sp, s_x2b, before)
                    sp.dma_start(n_x[0:b.rows, b.slot(6)], rows).then_inc(q_x[b.slot(6)], 16)
                if (b := node(SUMS_AT)) is not None:
                    sums = rows_of(aggr[0:N, :], b, NODES)
                    before, scattered = counts(b, b.at - 2, SCATTERED * (b.value + b.k // 6 + 1))
                    if not apart:
                        sp.wait_ge(q_scatter[(b.k // 2) % 3], scattered)
                    elif b.is_number(0):
                        for q in range(3):
                            sp.wait_ge(q_scatter[q], SCATTERED * len(range(q, NC, 3)))
                    reached(sp, s_nin, before)
                    sp.dma_start(n_aggr[0:b.rows, b.slot(3)], sums).then_inc(q_aggr[b.slot(3)], 16)
                if (b := node(SP_LAG)) is not None:
                    rows = rows_of(out, b, NODES)
                    finished, = counts(b, b.at + 1)
                    sp.wait_ge(s_nout, finished)
                    sp.dma_start(rows, n_out[0:b.rows, b.slot(2)]).then_inc(q_out[b.slot(2)], 16)

            sp.wait_ge(s_zeros, 1)
            branch(sp, 0, SP_LAG, step)
            for q in range(2):
                sp.wait_ge(q_out[q], 16 * len(range(q, NB, 2)))

        @block.gpsimd
        def _(pool):
            nc.gpsimd.memset(ident[:], 0.0).then_inc(s_const, 1)
            nc.gpsimd.memset(later[:], 1.0).then_inc(s_const, 1)
            nc.gpsimd.memset(minus_half[:], -0.5).then_inc(s_const, 1)
            nc.gpsimd.iota(spare[:], [[P, J]], base=N, channel_multiplier=1,
                           allow_small_or_imprecise_dtypes=True).then_inc(s_const, 1)
            nc.gpsimd.iota(o_high_limit[:], [[0, 1]], base=N, channel_multiplier=-2 * BLOCK,
                           allow_small_or_imprecise_dtypes=True).then_inc(s_const, 1)
            nc.gpsimd.iota(o_low_limit[:], [[0, 1]], base=ZERO_PARTS[1][0], channel_multiplier=-ZERO_ROWS,
                           allow_small_or_imprecise_dtypes=True).then_inc(s_const, 1)
            pool.wait_ge(s_const, 6)
            nc.gpsimd.affine_select(out=ident[:], in_=ident[:], compare_op=ALU.not_equal, fill=1.0,
                                    base=0, pattern=[[-1, P]], channel_multiplier=1).then_inc(s_const, 1)
            nc.gpsimd.affine_select(out=later[:, 0:P], in_=later[:, 0:P], compare_op=ALU.is_ge, fill=0.0,
                                    base=0, pattern=[[1, P]], channel_multiplier=-1).then_inc(s_const, 1)
            pool.wait_ge(s_param, ALL_PARAMS)
            pool.wait_ge(s_scaled_params, 2)

            last_node, last_sum, bound = (pool.alloc_register(n) for n in ("last_node", "last_sum", "bound"))
            pool.reg_mov(last_node, N - 2)
            pool.reg_mov(last_sum, AGGR_ROWS - 2)

            LAST_ZEROED = LEAD + NODE_TURN - 1 - EDGE_LAG

            def step(node, edge, halves, apart):
                if (b := node(1)) is not None:
                    r, s = b.rows, b.slot(6)
                    pool.wait_ge(s_nvar, b.at + 1)
                    nc.gpsimd.tensor_tensor(n_rstd[0:r, s], n_var[0:r, s],
                                            minus_half[0:r].rearrange("p (a j) -> p a j", j=J),
                                            ALU.pow).then_inc(s_nrstd, 1)
                if (b := node(2)) is not None:
                    r = b.rows
                    pool.wait_ge(s_nz, b.at + 1)
                    nc.gpsimd.tensor_tensor(n_zg[0:r, b.slot(2)], n_z[0:r, b.slot(2)], g1e_row[0:r],
                                            ALU.mult).then_inc(s_nzg, 1)
                    pool.wait_ge(s_nzg, b.at + 1)
                    pool.wait_ge(q_aggr[b.slot(3)], 16 * (b.uses(3) + 1))
                    reached(pool, s_tin, b.at - 1)
                    nc.gpsimd.tensor_tensor(n_in[0:r, b.slot(2)], n_zg[0:r, b.slot(2)], n_aggr[0:r, b.slot(3)],
                                            ALU.add).then_inc(s_nin, 1)
                if 0 in halves and (c := edge(0)) is not None:
                    r, s = c.rows, c.slot(3)
                    pool.wait_ge(q_cols[s], 16 * (c.uses(3) + 1))
                    reached(pool, s_erelu, c.at - 2)
                    pool.reg_add(bound, last_node, 1)
                    for j in range(J):
                        nc.gpsimd.indirect_dma_start(
                            out=e_x[0:r, s, j, :], out_offset=None, in_=x,
                            in_offset=bass.IndirectOffsetOnAxis(ap=e_cols[0:r, s, 0, j:j + 1], axis=0),
                            bounds_check=bound,
                        ).then_inc(q_gather[s], 16)
                if (b := node(4)) is not None:
                    r, s = b.rows, b.slot(6)
                    pool.wait_ge(s_var2, b.at + 1)
                    nc.gpsimd.tensor_tensor(n_rstd2[0:r, s], n_var2[0:r, s], minus_half[0:r, 0:J],
                                            ALU.pow).then_inc(s_rstd2, 1)
                if 0 in halves and (c := edge(2)) is not None:
                    r, s = c.rows, c.slot(3)
                    pool.wait_ge(q_attr[s], 16 * (c.uses(3) + 1))
                    reached(pool, s_esum, c.at - 2)
                    nc.gpsimd.tensor_tensor(e_attrb[0:r, s], e_attr[0:r, s], b1_row[0:r],
                                            ALU.add).then_inc(s_eattrb, 1)
                    pool.wait_ge(s_evar, c.at + 1)
                    nc.gpsimd.tensor_tensor(e_rstd[0:r, s], e_var[0:r, s],
                                            minus_half[0:r].rearrange("p (a j) -> p a j", j=J),
                                            ALU.pow).then_inc(s_erstd, 1)
                if 1 in halves and (c := edge(3)) is not None:
                    r, s = c.rows, c.slot(3)
                    pool.wait_ge(s_emerged, c.at + 1)
                    pool.wait_ge(s_eindex, c.at + 1)
                    if c.fixed and apart and c.k == 0:
                        for q in s_zeroed:
                            pool.wait_ge(q, 16)
                    if c.fixed and not apart and c.k < LAST_ZEROED:
                        for q in s_zeroed[c.k + 1 if c.k else 0:c.k + 2]:
                            pool.wait_ge(q, 16)
                    if c.fixed and not apart and c.k == LAST_ZEROED:
                        for q in s_zeroed[c.k + 1:]:
                            pool.wait_ge(q, 16)
                    if not c.is_number(0):
                        pool.wait_ge(q_scatter[(c.k - 1) % 3], SCATTERED * (c.value + (c.k - 1) // 3 + 1))
                    pool.reg_add(bound, last_sum, 1)
                    for j in range(J):
                        nc.gpsimd.indirect_dma_start(
                            out=aggr, out_offset=bass.IndirectOffsetOnAxis(
                                ap=e_index[0:r, s, j:j + 1], axis=0),
                            in_=e_merged[0:r, s, j, :], in_offset=None,
                            bounds_check=bound, compute_op=ALU.add,
                        ).then_inc(q_scatter[s], 16)

            branch(pool, EDGE_LAG, 4, step)

        @block.scalar
        def _(act):
            def per_row(to, of, scale, shift, rows):
                for j in range(J):
                    last = nc.scalar.activation(to[0:rows, j, :], of[0:rows, j, :], ACT.Identity,
                                                scale=scale[0:rows, j:j + 1],
                                                bias=0.0 if shift is None else shift[0:rows, j:j + 1])
                return last

            def gelu(b, ks):
                for k in ks:
                    act.wait_ge(s_f, b.at * KF + (k + 1))
                    if k == 0:
                        reached(act, s_fout, b.at)
                    nc.scalar.activation(n_act[:, k, :, 0:b.rows], p_f[k % 2][:, :, 0:b.rows],
                                         ACT.Gelu, bias=bf1_col[:, k:k + 1]).then_inc(s_act, 1)

            def step(node, edge, halves, apart):
                if (b := node(5)) is not None:
                    act.wait_ge(s_shift2, b.at + 1)
                    reached(act, s_tz2, b.at - 1)
                    per_row(n_z2[:, b.slot(2)], n_x2[:, b.slot(3)], n_rstd2[:, b.slot(6)],
                            n_shift2[:, b.slot(6)], b.rows).then_inc(s_z2, 1)
                if (b := node(3)) is not None:
                    act.wait_ge(s_tin, b.at + 1)
                    reached(act, s_g, b.at - 1)
                    nc.scalar.activation(n_inT[:, b.slot(2), :, 0:b.rows], p_in[:, :, 0:b.rows],
                                         ACT.Identity).then_inc(s_inT, 1)
                if (b := node(6)) is not None:
                    gelu(b, (0, 1))
                if (b := node(3)) is not None:
                    act.wait_ge(s_g, b.at + 1)
                    reached(act, s_gout, b.at - 1)
                    nc.scalar.activation(n_gT[:, b.slot(2), :, 0:b.rows], p_g[:, :, 0:b.rows], ACT.Relu,
                                         bias=bg1e_col[:, 0:1]).then_inc(s_gT, 1)
                if (b := node(6)) is not None:
                    gelu(b, (2, 3))
                if (b := node(5)) is not None:
                    act.wait_ge(s_tz2, b.at + 1)
                    reached(act, s_f, (b.at - 1) * KF)
                    nc.scalar.activation(n_z2T[:, b.slot(2), :, 0:b.rows], p_z2[:, :, 0:b.rows], ACT.Identity,
                                         bias=b2_col[:, 0:1], scale=g2_col[:, 0:1]).then_inc(s_z2T, 1)
                if 1 in halves and (c := edge(3)) is not None:
                    act.wait_ge(s_emm, c.at + 1)
                    if not (c.fixed and c.k < 3):
                        act.wait_ge(q_scatter[c.slot(3)], SCATTERED * c.uses(3))
                    nc.scalar.activation(e_merged[0:c.rows, c.slot(3)], p_merged[0:c.rows],
                                         ACT.Identity).then_inc(s_emerged, 1)
                if (b := node(1)) is not None:
                    act.wait_ge(s_nshift, b.at + 1)
                    reached(act, s_nzg, b.at - 1)
                    per_row(n_z[:, b.slot(2)], n_relu[:, b.slot(3)], n_rstd[:, b.slot(6), 1],
                            n_shift[:, b.slot(6)], b.rows).then_inc(s_nz, 1)
                    reached(act, s_x2, b.at - 5)
                    per_row(n_h[:, b.slot(6)], n_relu[:, b.slot(3)], n_rstd[:, b.slot(6), 0],
                            None, b.rows).then_inc(s_nh, 1)
                if 1 in halves and (c := edge(2)) is not None:
                    act.wait_ge(s_esum, c.at + 1)
                    reached(act, s_emm, c.at - 2)
                    nc.scalar.activation(e_msg[0:c.rows, c.slot(3)], e_sum[0:c.rows, c.slot(3)],
                                         ACT.Relu).then_inc(s_emsg, 1)

            act.wait_ge(s_bias, 1)
            branch(act, EDGE_LAG, 6, step)

        @block.vector
        def _(dve):
            nc.vector.memset(zeros[:], 0.0).then_inc(s_zeros, 1)
            nc.vector.memset(ones[:], 1.0).then_inc(s_ones, 1)
            nc.vector.memset(ones_col[:], 1.0).then_inc(s_ones, 1)
            nc.vector.memset(bias_rows[:], 0.0).then_inc(s_rows, 1)

            dve.wait_ge(s_order_in, 16)
            nc.vector.tensor_reduce(o_high[:], o_dst[:], mybir.AxisListType.X, ALU.max).then_inc(s_bounds, 1)
            nc.vector.tensor_reduce(o_low[:], o_dst[:], mybir.AxisListType.X, ALU.min).then_inc(s_bounds, 1)
            dve.wait_ge(s_bounds, 2)
            dve.wait_ge(s_const, 6)
            nc.vector.tensor_tensor(o_above[:], o_high[:], o_high_limit[:], ALU.is_ge).then_inc(s_order, 1)
            nc.vector.tensor_tensor(o_below[:], o_low[:], o_low_limit[:], ALU.is_lt).then_inc(s_order, 1)
            dve.wait_ge(s_order, 2)
            nc.vector.tensor_tensor(o_bad[:], o_above[:], o_below[:], ALU.add).then_inc(s_order, 1)
            dve.wait_ge(s_bad, 1)
            nc.vector.tensor_copy(o_flag[:], p_in[0:1, 0, 0:1]).then_inc(s_flag, 1)

            dve.wait_ge(s_param, ALL_PARAMS)
            nc.vector.tensor_scalar(eps_col[:], eps_col[:], 1.0, None, ALU.add).then_inc(s_eps, 1)
            dve.wait_ge(s_eps, 1)
            nc.vector.tensor_scalar(b1e_col[:], b1_col[:], eps_col[:, 0:1], None, ALU.mult).then_inc(s_scaled_params, 1)
            nc.vector.tensor_scalar(g1e_row[:], g1_row[:], eps_col[:, 0:1], None, ALU.mult).then_inc(s_scaled_params, 1)
            nc.vector.tensor_copy(bias_part[:, 0], bias_row[:]).then_inc(s_part, 1)
            dve.wait_ge(s_part, 1)
            nc.vector.tensor_tensor(bias_rest[:], bias_row[:], bias_part[:, 0], ALU.subtract).then_inc(s_part, 1)
            dve.wait_ge(s_part, 2)
            nc.vector.tensor_copy(bias_part[:, 1], bias_rest[:]).then_inc(s_part, 1)
            dve.wait_ge(s_part, 3)
            nc.vector.tensor_tensor(bias_row[:], bias_rest[:], bias_part[:, 1], ALU.subtract).then_inc(s_part, 1)
            dve.wait_ge(s_part, 4)
            nc.vector.tensor_copy(bias_part[:, 2], bias_row[:]).then_inc(s_part, 1)
            dve.wait_ge(s_part, 5)
            dve.wait_ge(s_rows, 1)
            for i in range(3):
                for j in range(J):
                    last = nc.vector.tensor_copy(bias_rows[32 * i:32 * i + 1, :, j, :],
                                                 bias_part[32 * i:32 * i + 1, i])
            last.then_inc(s_rows, 1)
            dve.wait_ge(s_b1g, 1)
            nc.vector.tensor_tensor(bg1e_col[:], p_g[:, 0, 0:1], bg1_col[:], ALU.add).then_inc(s_bias, 1)
            dve.wait_ge(s_const, 8)

            def stats(to, of, rows, done):
                for j in range(J):
                    last = nc.vector.bn_stats(to[0:rows, j, :], of[0:rows, j, :])
                last.then_inc(done, 1)

            def moments(to, of, rows, done):
                for j in range(J):
                    last = nc.vector.bn_aggr(to[0:rows, j, :], of[0:rows, j, :])
                last.then_inc(done, 1)

            def centred_relu(to, of, mom, rows, done):
                for j in range(J):
                    last = nc.vector.tensor_scalar(to[0:rows, j, :], of[0:rows, j, :], mom[0:rows, j, 0:1],
                                                   0.0, ALU.subtract, ALU.max)
                last.then_inc(done, 1)

            def both_variances(var, mom, rows, between, at, done):
                nc.vector.tensor_scalar(var[0:rows, 0, :], mom[0:rows, 0, :, 1], EPS, None,
                                        ALU.add).then_inc(between, 1)
                dve.wait_ge(between, at + 1)
                nc.vector.scalar_tensor_tensor(var[0:rows, 1, :], var[0:rows, 0, :], EPS,
                                               mom[0:rows, 1, :, 1], ALU.mult, ALU.add).then_inc(done, 1)

            def edges_first_half(c):
                s, r = c.slot(3), c.rows
                dve.wait_ge(q_gather[s], 16 * J * (c.uses(3) + 1))
                stats(e_stat[:, s, 0], e_x[:, s], r, s_estat)
                dve.wait_ge(s_estat, c.at + 1)
                nc.vector.tensor_copy(e_dstf[0:r, s], e_cols[0:r, s, 1, :]).then_inc(s_ecopy, 1)
                moments(e_mom[:, s, 0], e_stat[:, s, 0], r, s_emom)
                dve.wait_ge(s_ecopy, c.at + 1)
                nc.vector.tensor_tensor(e_toward[0:r, s], spare[0:r], e_dstf[0:r, s],
                                        ALU.subtract).then_inc(s_etoward, 1)
                dve.wait_ge(s_emom, c.at + 1)
                centred_relu(e_relu[:, s], e_x[:, s], e_mom[:, s, 0], r, s_erelu)
                dve.wait_ge(q_dst[s], 16 * (c.uses(3) + 1))
                reached(dve, s_emm, c.at - 2)
                for a in range(J):
                    w = (J - a) * P
                    last = nc.vector.scalar_tensor_tensor(
                        e_match[0:r, s, MATCH_AT[a]:MATCH_AT[a] + w], e_dst[0:r, s, a * P:BLOCK],
                        e_dstf[0:r, s, a:a + 1], later[0:r, 0:w], ALU.is_equal, ALU.mult,
                        accum_out=e_count[0:r, s, a:a + 1])
                last.then_inc(s_ematch, 1)

            def edges_second_half(c):
                s, r = c.slot(3), c.rows
                dve.wait_ge(s_erelu, c.at + 1)
                stats(e_stat[:, s, 1], e_relu[:, s], r, s_estatu)
                dve.wait_ge(s_ematch, c.at + 1)
                dve.wait_ge(s_etoward, c.at + 1)
                dve.wait_ge(s_estatu, c.at + 1)
                nc.vector.scalar_tensor_tensor(e_extra[0:r, s], e_count[0:r, s], 1.5, e_toward[0:r, s],
                                               ALU.is_gt, ALU.mult).then_inc(s_eextra, 1)
                moments(e_mom[:, s, 1], e_stat[:, s, 1], r, s_emomu)
                if not (c.fixed and c.k < 3):
                    dve.wait_ge(q_scatter[s], SCATTERED * c.uses(3))
                dve.wait_ge(s_eextra, c.at + 1)
                nc.vector.tensor_tensor(e_index[0:r, s], e_dstf[0:r, s], e_extra[0:r, s],
                                        ALU.add).then_inc(s_eindex, 1)
                dve.wait_ge(s_emomu, c.at + 1)
                both_variances(e_var[:, s], e_mom[:, s], r, s_evar0, c.at, s_evar)
                for j in range(J):
                    last = nc.vector.scalar_tensor_tensor(
                        e_scaled[0:r, s, j, :], e_relu[0:r, s, j, :], e_mom[0:r, s, 1, j, 0:1],
                        g1_row[0:r, j, :], ALU.subtract, ALU.mult)
                last.then_inc(s_escaled, 1)

            def edges_sum(c):
                s, r = c.slot(3), c.rows
                dve.wait_ge(s_escaled, c.at + 1)
                dve.wait_ge(s_erstd, c.at + 1)
                dve.wait_ge(s_eattrb, c.at + 1)
                reached(dve, s_emsg, c.at - 2)
                for j in range(J):
                    last = nc.vector.scalar_tensor_tensor(
                        e_sum[0:r, s, j, :], e_scaled[0:r, s, j, :], e_rstd[0:r, s, 1, j:j + 1],
                        e_attrb[0:r, s, j, :], ALU.mult, ALU.add)
                last.then_inc(s_esum, 1)

            def step(node, edge, halves, apart):
                first, second, fifth, sixth = node(0), node(1), node(4), node(5)
                if (b := sixth) is not None:
                    r, s = b.rows, b.slot(6)
                    dve.wait_ge(s_rstd2, b.at + 1)
                    nc.vector.scalar_tensor_tensor(n_shift2[0:r, s], n_mom2[0:r, s, :, 0], -1.0, n_rstd2[0:r, s],
                                                   ALU.mult, ALU.mult).then_inc(s_shift2, 1)
                if (b := fifth) is not None:
                    r, s = b.rows, b.slot(6)
                    dve.wait_ge(s_gout, b.at + 1)
                    dve.wait_ge(s_nh, b.at + 1)
                    reached(dve, s_z2, b.at - 2)
                    nc.vector.tensor_tensor(n_x2[0:r, b.slot(3)], p_gout[0:r], n_h[0:r, s],
                                            ALU.add).then_inc(s_x2, 1)
                if (b := node(7)) is not None:
                    r = b.rows
                    dve.wait_ge(s_fout, b.at + 1)
                    if not (b.fixed and b.k < 2):
                        dve.wait_ge(q_out[b.slot(2)], 16 * b.uses(2))
                    nc.vector.tensor_tensor(n_out[0:r, b.slot(2)], p_out[0:r], n_x2b[0:r, b.slot(6)],
                                            ALU.add).then_inc(s_nout, 1)
                if (b := first) is not None:
                    dve.wait_ge(q_x[b.slot(6)], 16 * (b.uses(6) + 1))
                    stats(n_stat[:, b.slot(6), 0], n_x[:, b.slot(6)], b.rows, s_nstat)
                    dve.wait_ge(s_nstat, b.at + 1)
                if (b := fifth) is not None:
                    dve.wait_ge(s_x2, b.at + 1)
                    stats(n_stat2[:, b.slot(6)], n_x2[:, b.slot(3)], b.rows, s_stat2)
                if (b := first) is not None:
                    moments(n_mom[:, b.slot(6), 0], n_stat[:, b.slot(6), 0], b.rows, s_nmom)
                if (b := fifth) is not None:
                    dve.wait_ge(s_stat2, b.at + 1)
                if (b := first) is not None:
                    dve.wait_ge(s_nmom, b.at + 1)
                    reached(dve, s_nh, b.at - 2)
                    centred_relu(n_relu[:, b.slot(3)], n_x[:, b.slot(6)], n_mom[:, b.slot(6), 0], b.rows, s_nrelu)
                if (b := fifth) is not None:
                    r, s = b.rows, b.slot(6)
                    moments(n_mom2[:, s], n_stat2[:, s], r, s_mom2)
                    dve.wait_ge(s_mom2, b.at + 1)
                    nc.vector.tensor_scalar(n_var2[0:r, s], n_mom2[0:r, s, :, 1], EPS, None,
                                            ALU.add).then_inc(s_var2, 1)
                if (b := first) is not None:
                    dve.wait_ge(s_nrelu, b.at + 1)
                    stats(n_stat[:, b.slot(6), 1], n_relu[:, b.slot(3)], b.rows, s_nstatu)
                if (b := second) is not None:
                    r, s = b.rows, b.slot(6)
                    dve.wait_ge(s_nrstd, b.at + 1)
                    nc.vector.scalar_tensor_tensor(n_shift[0:r, s], n_mom[0:r, s, 1, :, 0], -1.0, n_rstd[0:r, s, 1],
                                                   ALU.mult, ALU.mult).then_inc(s_nshift, 1)
                if (b := first) is not None:
                    dve.wait_ge(s_nstatu, b.at + 1)
                if (b := fifth) is not None:
                    r, s = b.rows, b.slot(6)
                    nc.vector.tensor_tensor(n_x2b[0:r, s], n_x2[0:r, b.slot(3)], n_x[0:r, s],
                                            ALU.add).then_inc(s_x2b, 1)
                if 0 in halves and (c := edge(1)) is not None:
                    edges_first_half(c)
                if 1 in halves and (c := edge(1)) is not None:
                    edges_second_half(c)
                if (b := first) is not None:
                    moments(n_mom[:, b.slot(6), 1], n_stat[:, b.slot(6), 1], b.rows, s_nmomu)
                    dve.wait_ge(s_nmomu, b.at + 1)
                    both_variances(n_var[:, b.slot(6)], n_mom[:, b.slot(6)], b.rows, s_nvar0, b.at, s_nvar)
                if 1 in halves and (c := edge(2)) is not None:
                    edges_sum(c)

            branch(dve, EDGE_LAG, NODE_LAG, step)

        @block.tensor
        def _(pe):
            pe.wait_ge(s_order, 3)
            pe.wait_ge(s_ones, 2)
            nc.tensor.matmul(p_in[0:1, 0, 0:1], o_bad[:], ones_col[0:NC, :], start=True, stop=True).then_inc(s_bad, 1)
            pe.wait_ge(s_scaled_params, 1)
            nc.tensor.matmul(p_g[:, 0, 0:1], wg1[:], b1e_col[:], start=True, stop=True).then_inc(s_b1g, 1)
            pe.wait_ge(s_bias, 1)
            pe.wait_ge(s_const, 8)
            pe.wait_ge(s_rows, 2)

            def add_bias(to, which):
                nc.tensor.matmul(to[:], ones[:], bias_rows[:, which], start=True, stop=False,
                                 skip_group_check=True)

            def first_product(b, ks):
                for k in ks:
                    reached(pe, s_act, b.at * KF + k - 1)
                    nc.tensor.matmul(p_f[k % 2][:, :, 0:b.rows], wf1[:, k * P:(k + 1) * P],
                                     n_z2T[:, b.slot(2), :, 0:b.rows], start=True, stop=True).then_inc(s_f, 1)

            def step(node, edge, halves, apart):
                fourth, sixth, seventh = node(3), node(5), node(6)
                if (b := fourth) is not None:
                    pe.wait_ge(s_nin, b.at + 1)
                    reached(pe, s_inT, b.at)
                    for j in range(J):
                        last = nc.tensor.transpose(p_in[:, j, 0:b.rows], n_in[0:b.rows, b.slot(2), j, :],
                                                   ident[0:b.rows, 0:b.rows])
                    last.then_inc(s_tin, 1)
                if (b := seventh) is not None:
                    pe.wait_ge(s_z2T, b.at + 1)
                    first_product(b, (0, 1))
                if (b := fourth) is not None:
                    pe.wait_ge(s_inT, b.at + 1)
                    reached(pe, s_gT, b.at)
                    nc.tensor.matmul(p_g[:, :, 0:b.rows], wg1[:], n_inT[:, b.slot(2), :, 0:b.rows],
                                     start=True, stop=True).then_inc(s_g, 1)
                if (b := seventh) is not None:
                    first_product(b, (2, 3))
                if (b := fourth) is not None:
                    reached(pe, s_x2, b.at)
                    add_bias(p_gout, 0)
                    pe.wait_ge(s_gT, b.at + 1)
                    for j in range(J):
                        last = nc.tensor.matmul(p_gout[0:b.rows, j, :], n_gT[:, b.slot(2), j, 0:b.rows], wg2[:],
                                                start=False, stop=True, skip_group_check=True)
                    last.then_inc(s_gout, 1)
                if (b := sixth) is not None:
                    pe.wait_ge(s_z2, b.at + 1)
                    reached(pe, s_z2T, b.at)
                    for j in range(J):
                        last = nc.tensor.transpose(p_z2[:, j, 0:b.rows], n_z2[0:b.rows, b.slot(2), j, :],
                                                   ident[0:b.rows, 0:b.rows])
                    last.then_inc(s_tz2, 1)
                if (b := seventh) is not None:
                    reached(pe, s_nout, b.at)
                    add_bias(p_out, 1)
                    for k in range(KF):
                        pe.wait_ge(s_act, b.at * KF + (k + 1))
                        for j in range(J):
                            last = nc.tensor.matmul(p_out[0:b.rows, j, :], n_act[:, k, j, 0:b.rows], wf2[:, k, :],
                                                    start=False, stop=(k == KF - 1), skip_group_check=True)
                    last.then_inc(s_fout, 1)
                if 0 in halves and (c := edge(3)) is not None:
                    s, r = c.slot(3), c.rows
                    pe.wait_ge(s_ematch, c.at + 1)
                    pe.wait_ge(s_emsg, c.at + 1)
                    reached(pe, s_emerged, c.at)
                    for i in range(J):
                        for a in range(i + 1):
                            m = MATCH_AT[a] + (i - a) * P
                            last = nc.tensor.matmul(p_merged[0:r, i, :], e_match[0:r, s, m:m + r],
                                                    e_msg[0:r, s, a, :], start=(a == 0), stop=(a == i))
                    last.then_inc(s_emm, 1)

            branch(pe, EDGE_LAG, 6, step)


_WEIGHTS = ["g1", "b1", "g2", "b2", "eps_gin", "Wg1", "bg1", "Wg2", "bg2", "Wf1", "bf1", "Wf2", "bf2"]


def kernel(**inputs):
    import numpy as _np
    import concourse.bacc as _bacc
    from concourse import mybir as _mybir
    from concourse.bass_utils import run_bass_kernel_spmd as _run

    x = _np.ascontiguousarray(inputs["x"])
    attr = _np.ascontiguousarray(inputs["edge_attr_128"])
    edges = attr.shape[0]
    short = edges % BLOCK

    def in_chunks(a, fill):
        a = _np.asarray(a)
        first = _np.pad(a[:short], (0, BLOCK - short), constant_values=fill).reshape(1, BLOCK)
        return _np.concatenate([a[short:].reshape(-1, BLOCK)[::-1], first]).reshape(-1, P, J)

    src, dst = in_chunks(inputs["src"], 0), in_chunks(inputs["dst"], -1)
    arrays = {"in_x": x, "in_attr": attr,
              "in_edge_cols": _np.ascontiguousarray(_np.stack([src, dst], 2).reshape(-1, 2 * J)),
              "in_dst_rows": _np.ascontiguousarray(dst.transpose(0, 2, 1).reshape(-1, BLOCK))}
    for name in _WEIGHTS:
        arrays[f"in_{name}"] = _np.ascontiguousarray(inputs[f"L0_gnn_{name}"])
    arrays["in_eps_gin"] = arrays["in_eps_gin"].reshape(1)

    nc = _bacc.Bacc("TRN2", target_bir_lowering=False, num_devices=1)
    args = [nc.dram_tensor(n, a.shape, _mybir.dt.from_np(a.dtype), kind="ExternalInput").ap()
            for n, a in arrays.items()]
    out = nc.dram_tensor("out_dram", x.shape, _mybir.dt.float32, kind="ExternalOutput").ap()
    gnn_kernel(nc, *args, out)
    r = _run(nc, [arrays], core_ids=[0])
    return r.results[0]["out_dram"]
```

```python
from contextlib import ExitStack

import concourse.bass as bass
from concourse import mybir

ALU = mybir.AluOpType
ACT = mybir.ActivationFunctionType
F32 = mybir.dt.float32
I32 = mybir.dt.int32

BF16 = mybir.dt.bfloat16

P = 128
J = 4
BLOCK = P * J
NODE_TURN = 6
EDGE_TURN = 3
EPS = 1e-5

EDGE_LAG = 3
NODE_LAG = 7
SP_LAG = 9
SUMS_AT = 2
LEAD = 3


class Item:

    def __init__(self, value, unroll, k, rows):
        self.value, self.unroll, self.k, self.rows = value, unroll, k, rows
        self.at = value * unroll + k
        self.fixed = isinstance(value, int)

    def slot(self, depth):
        return self.k % depth

    def uses(self, depth):
        return self.value * (self.unroll // depth) + self.k // depth

    def is_number(self, n):
        return self.fixed and self.k == n


class Work:

    def __init__(self, count, tail_rows, unroll):
        self.count, self.tail_rows, self.unroll = count, tail_rows, unroll

    def at_step(self, t):
        def item_of(o):
            if t - o < 0 or t - o >= self.count:
                return None
            return Item(0, self.unroll, t - o, self.tail_rows if t - o == self.count - 1 else P)
        return item_of

    def in_loop(self, n, k):
        return lambda o: Item(n, self.unroll, k - o, P)


def nothing(o):
    return None


def edges_then_nodes(eng, edges, nodes, edge_lag, node_lag, step):
    first, last = 2, (edges.count - 2) // EDGE_TURN
    for t in range(LEAD, first * EDGE_TURN):
        step(nothing, edges.at_step(t), (0, 1), True)
    with eng.Fori(first, last) as n:
        for k in range(EDGE_TURN):
            step(nothing, edges.in_loop(n, k), (0, 1), True)
    for t in range(last * EDGE_TURN, edges.count + edge_lag):
        step(nothing, edges.at_step(t), (0, 1), True)
    first, last = 2, (nodes.count - 1) // NODE_TURN
    for t in range(-1, first * NODE_TURN):
        step(nodes.at_step(t), nothing, (), True)
    with eng.Fori(first, last) as n:
        for k in range(NODE_TURN):
            step(nodes.in_loop(n, k), nothing, (), True)
    for t in range(last * NODE_TURN, nodes.count + node_lag):
        step(nodes.at_step(t), nothing, (), True)


def edges_beside_nodes(eng, edges, nodes, edge_lag, node_lag, step):
    def peeled(t):
        step(nodes.at_step(t), edges.at_step(LEAD + (t + 1) // 2), ((t + 1) % 2,), False)

    first = 2
    last = 2 * (edges.count - 2 - LEAD) // NODE_TURN
    for t in range(-1, first * NODE_TURN):
        peeled(t)
    with eng.Fori(first, last) as n:
        for k in range(NODE_TURN):
            step(nodes.in_loop(n, k), edges.in_loop(n, LEAD + (k + 1) // 2), ((k + 1) % 2,), False)
    for t in range(last * NODE_TURN, nodes.count + node_lag):
        peeled(t)


def reached(eng, sem, value):
    if isinstance(value, int) and value <= 0:
        return
    eng.wait_ge(sem, value)


def gnn_kernel(nc, x, edge_attr, edge_cols, dst_rows, g1, b1, g2, b2, eps_gin,
               Wg1, bg1, Wg2, bg2, Wf1, bf1, Wf2, bf2, out):
    N, D = x.shape
    E = edge_attr.shape[0]
    DF = Wf1.shape[1]
    KF = DF // P
    NB, NC = -(-N // BLOCK), -(-E // BLOCK)
    NB_TAIL, NC_TAIL = (N - (NB - 1) * BLOCK) // J, (E - (NC - 1) * BLOCK) // J
    assert LEAD <= EDGE_LAG
    assert D == P and NB_TAIL * J + (NB - 1) * BLOCK == N and NC_TAIL * J + (NC - 1) * BLOCK == E
    NODES, EDGES = Work(NB, NB_TAIL, NODE_TURN), Work(NC, NC_TAIL, EDGE_TURN)

    ZERO_W = 1024
    ZERO_ROWS = 4096
    AGGR_ROWS = -(-(N + BLOCK) // ZERO_W) * ZERO_W
    aggr = nc.dram_tensor("aggr_sums", (AGGR_ROWS, D), F32, kind="Internal").ap()
    FINE_ROWS = 6 * ZERO_ROWS
    ZERO_PARTS = ([(hi - ZERO_ROWS // 2, hi) for hi in range(AGGR_ROWS, AGGR_ROWS - FINE_ROWS, -ZERO_ROWS // 2)]
                  + [(max(0, hi - ZERO_ROWS), hi) for hi in range(AGGR_ROWS - FINE_ROWS, 0, -ZERO_ROWS)])

    def zeroed_for(c):
        return sum(hi > AGGR_ROWS - (c + 2) * (ZERO_ROWS // 2) for _, hi in ZERO_PARTS)


    with ExitStack() as ctx:
        def sb(name, shape, dt=F32):
            return ctx.enter_context(nc.sbuf_tensor(name, shape, dt))

        def pb(name):
            return ctx.enter_context(nc.psum_tensor(name, [P, J, P], F32))

        def sem(name):
            return ctx.enter_context(nc.semaphore(name))

        def ring_sems(name, depth):
            return [sem(f"{name}{i}") for i in range(depth)]

        ident = sb("ident", [P, P])
        later = sb("later", [P, BLOCK])
        spare = sb("spare", [P, J])
        zeros = sb("zeros", [P, ZERO_W])
        ones = sb("ones", [P, P], BF16)
        ones_col = sb("ones_col", [P, 1])
        minus_half = sb("minus_half", [P, 2 * J])
        g1_row = sb("g1_row", [P, J, D])
        g1e_row = sb("g1e_row", [P, J, D])
        b1_row = sb("b1_row", [P, J, D])
        bias_row = sb("bias_row", [P, 2, D])
        bias_rest = sb("bias_rest", [P, 2, D])
        bias_part = sb("bias_part", [P, 3, 2, D], BF16)
        bias_rows = sb("bias_rows", [P, 2, J, D], BF16)
        eps_col = sb("eps_col", [P, 1])
        b1_col = sb("b1_col", [P, 1])
        b1e_col = sb("b1e_col", [P, 1])
        bg1_col = sb("bg1_col", [P, 1])
        bg1e_col = sb("bg1e_col", [P, 1])
        g2_col = sb("g2_col", [P, 1])
        b2_col = sb("b2_col", [P, 1])
        bf1_col = sb("bf1_col", [P, KF])
        wg1 = sb("wg1", [P, D])
        wg2 = sb("wg2", [P, D])
        wf1 = sb("wf1", [P, DF])
        wf2 = sb("wf2", [P, KF, D])
        o_dst = sb("o_dst", [NC, BLOCK], I32)
        o_high, o_low, o_high_limit, o_low_limit, o_above, o_below, o_bad = (
            sb(f"o_{n}", [NC, 1]) for n in ("high", "low", "high_limit", "low_limit", "above", "below", "bad"))
        o_flag = sb("o_flag", [1, 1], I32)

        e_x, e_attr, e_relu, e_scaled, e_attrb, e_sum, e_msg, e_merged = (
            sb(f"e_{n}", [P, 3, J, D]) for n in ("x", "attr", "relu", "scaled", "attrb", "sum", "msg", "merged"))
        e_cols = sb("e_cols", [P, 3, 2, J], I32)
        e_dst = sb("e_dst", [P, 3, BLOCK], I32)
        e_dstf, e_toward, e_count, e_extra = (
            sb(f"e_{n}", [P, 3, J]) for n in ("dstf", "toward", "count", "extra"))
        e_match = sb("e_match", [P, 3, J * (J + 1) // 2 * P])
        e_index = sb("e_index", [P, 3, J], I32)
        e_stat = sb("e_stat", [P, 3, 2, J, 6])
        e_mom = sb("e_mom", [P, 3, 2, J, 2])
        e_var = sb("e_var", [P, 3, 2, J])
        e_rstd = sb("e_rstd", [P, 3, J])

        n_x, n_h, n_x2b = (sb(f"n_{n}", [P, 6, J, D]) for n in ("x", "h", "x2b"))
        n_aggr, n_relu, n_x2 = (sb(f"n_{n}", [P, 3, J, D]) for n in ("aggr", "relu", "x2"))
        n_z, n_zg, n_in, n_z2, n_out = (sb(f"n_{n}", [P, 2, J, D]) for n in ("z", "zg", "in", "z2", "out"))
        n_inT, n_gT, n_z2T = (sb(f"n_{n}", [P, 2, J, P]) for n in ("inT", "gT", "z2T"))
        n_act = sb("n_act", [P, KF, J, P])
        n_stat = sb("n_stat", [P, 6, 2, J, 6])
        n_mom = sb("n_mom", [P, 6, 2, J, 2])
        n_var, n_rstd = (sb(f"n_{n}", [P, 6, 2, J]) for n in ("var", "rstd"))
        n_stat2 = sb("n_stat2", [P, 6, J, 6])
        n_mom2 = sb("n_mom2", [P, 6, J, 2])
        n_shift, n_var2, n_rstd2, n_shift2 = (
            sb(f"n_{n}", [P, 6, J]) for n in ("shift", "var2", "rstd2", "shift2"))

        p_in, p_g, p_gout, p_z2, p_out, p_merged = (
            pb(f"p_{n}") for n in ("in", "g", "gout", "z2", "out", "merged"))
        p_f = [pb(f"p_f{i}") for i in range(2)]

        (s_edge_param, s_node_param, s_const, s_ones, s_eps, s_scaled_params, s_b1g, s_bias, s_zeros, s_part, s_rows,
         s_order_in, s_bounds, s_order, s_bad, s_flag) = (sem(f"s_{n}") for n in (
             "edge_param", "node_param", "const", "ones", "eps", "scaled_params", "b1g", "bias", "zeros", "part", "rows",
             "order_in", "bounds", "order", "bad", "flag"))
        s_zeroed = [sem(f"s_zeroed{i}") for i in range(len(ZERO_PARTS))]
        q_attr, q_cols, q_dst, q_gather, q_scatter = (
            ring_sems(f"q_{n}", 3) for n in ("attr", "cols", "dst", "gather", "scatter"))
        (s_ecopy, s_etoward, s_estat, s_emom, s_erelu, s_estatu, s_emomu, s_evar0, s_evar, s_erstd,
         s_escaled, s_eattrb, s_esum, s_emsg, s_ematch, s_eextra, s_eindex, s_emm, s_emerged) = (
            sem(f"s_e{n}") for n in (
                "copy", "toward", "stat", "mom", "relu", "statu", "momu", "var0", "var", "rstd",
                "scaled", "attrb", "sum", "msg", "match", "extra", "index", "mm", "merged"))
        q_x, q_aggr, q_out = ring_sems("q_x", 6), ring_sems("q_aggr", 3), ring_sems("q_out", 2)
        (s_nstat, s_nmom, s_nrelu, s_nstatu, s_nmomu, s_nvar0, s_nvar, s_nrstd, s_nshift, s_nz, s_nh,
         s_nzg, s_nin, s_tin, s_inT, s_g, s_gT, s_gout, s_x2, s_stat2, s_mom2, s_var2, s_rstd2,
         s_shift2, s_x2b, s_z2, s_tz2, s_z2T, s_f, s_act, s_fout, s_nout) = (
            sem(f"s_n{n}") for n in (
                "stat", "mom", "relu", "statu", "momu", "var0", "var", "rstd", "shift", "z", "h",
                "zg", "in", "tin", "inT", "g", "gT", "gout", "x2", "stat2", "mom2", "var2", "rstd2",
                "shift2", "x2b", "z2", "tz2", "z2T", "f", "act", "fout", "out"))

        def rows_of(dram, item, work):
            if item.is_number(work.count - 1):
                start = 0
            else:
                start = item.value * (-item.unroll * BLOCK * D) + (dram.shape[0] - BLOCK * (item.k + 1)) * D
            return dram.rearrange("n d -> (n d)")[bass.ds(start, item.rows * J * D)].rearrange(
                "(p j d) -> p j d", j=J, d=D)

        def row(vector, times=None):
            if times is None:
                return vector.unsqueeze(0).to_broadcast([P, D])
            return vector.unsqueeze(0).unsqueeze(0).to_broadcast([P, times, D])

        EDGE_PARAMS = [(g1_row[:], row(g1, J)), (b1_row[:], row(b1, J))]
        NODE_PARAMS = [
            (bias_row[:, 0], row(bg2)), (bias_row[:, 1], row(bf2)),
            (eps_col[:], eps_gin.unsqueeze(0).to_broadcast([P, 1])),
            (b1_col[:], b1.unsqueeze(1)), (bg1_col[:], bg1.unsqueeze(1)),
            (g2_col[:], g2.unsqueeze(1)), (b2_col[:], b2.unsqueeze(1)),
            (bf1_col[:], bf1.rearrange("(k p) -> p k", p=P)),
            (wg1[:], Wg1), (wg2[:], Wg2), (wf1[:], Wf1),
            (wf2[:], Wf2.rearrange("(k p) d -> p k d", p=P)),
        ]
        SCATTERED = 16 * J
        MATCH_AT = [sum(J - i for i in range(a)) * P for a in range(J)]

        def first_chunks(step, *times):
            for t in times:
                step(nothing, EDGES.at_step(t), (0, 1), False)

        def branch(eng, edge_lag, node_lag, step):
            eng.wait_ge(s_flag, 1)
            unordered = eng.alloc_register("unordered")
            eng.reg_load(unordered, o_flag[0:1, 0:1])
            with eng.If_eq(unordered, 0):
                edges_beside_nodes(eng, EDGES, NODES, edge_lag, node_lag, step)
            with eng.Else():
                edges_then_nodes(eng, EDGES, NODES, edge_lag, node_lag, step)

        block = ctx.enter_context(nc.Block())

        @block.sync
        def _(sp):
            count_registers = [sp.alloc_register(f"count{i}") for i in range(2)]

            def counts(item, *values):
                if item.fixed:
                    return values
                for register, v in zip(count_registers, values):
                    sp.reg_mov(register, v)
                sp.wait_ge(s_flag, 1)
                return count_registers[0:len(values)]

            def zero_parts_begun(t):
                return 2 if t < 0 else min(len(ZERO_PARTS), 5 + t + max(0, t - 4))

            def set_to_zero(parts):
                for part in parts:
                    lo, hi = ZERO_PARTS[part]
                    a = (hi - lo) * D // P // ZERO_W
                    sp.dma_start(aggr[lo:hi, :].rearrange("(p a r) d -> p a (r d)", p=P, a=a),
                                 zeros[:].unsqueeze(1).to_broadcast([P, a, ZERO_W])).then_inc(s_zeroed[part], 16)

            def load_ends(c):
                s = c.slot(3)
                cols = edge_cols.rearrange("n a -> (n a)")[bass.ds(
                    c.value * (c.unroll * BLOCK * 2) + c.k * BLOCK * 2,
                    c.rows * 2 * J)].rearrange("(p a) -> p a", p=c.rows)
                destinations = dst_rows.rearrange("c i -> (c i)")[bass.ds(
                    c.value * (c.unroll * BLOCK) + c.k * BLOCK, BLOCK)]
                before, gathered = counts(c, c.at - 2, c.uses(3) * 16 * J)
                reached(sp, s_ematch, before)
                reached(sp, s_eindex, before)
                reached(sp, s_etoward, before)
                reached(sp, q_gather[s], gathered)
                sp.dma_start(e_cols[0:c.rows, s].rearrange("p a j -> p (a j)"), cols).then_inc(q_cols[s], 16)
                sp.dma_start(e_dst[:, s, :], destinations.unsqueeze(0).to_broadcast([P, BLOCK])
                             ).then_inc(q_dst[s], 16)

            def load_x(b):
                rows = rows_of(x, b, NODES)
                before, = counts(b, b.at - 5)
                reached(sp, s_x2b, before)
                sp.dma_start(n_x[0:b.rows, b.slot(6)], rows).then_inc(q_x[b.slot(6)], 16)

            def step(node, edge, halves, apart):
                if (c := edge(0)) is not None and apart and c.is_number(LEAD):
                    set_to_zero(range(zero_parts_begun(0), len(ZERO_PARTS)))
                if 0 in halves and (c := edge(0)) is not None:
                    s = c.slot(3)
                    attributes = rows_of(edge_attr, c, EDGES)
                    before, = counts(c, c.at - 2)
                    reached(sp, s_eattrb, before)
                    sp.dma_start(e_attr[0:c.rows, s], attributes).then_inc(q_attr[s], 16)
                if 1 in halves and (c := edge(-1)) is not None:
                    load_ends(c)
                if (b := node(SP_LAG)) is not None:
                    rows = rows_of(out, b, NODES)
                    finished, = counts(b, b.at + 1)
                    sp.wait_ge(s_nout, finished)
                    sp.dma_start(rows, n_out[0:b.rows, b.slot(2)]).then_inc(q_out[b.slot(2)], 16)
                if (b := node(SUMS_AT)) is not None:
                    sums = rows_of(aggr[0:N, :], b, NODES)
                    before, scattered = counts(b, b.at - 2, SCATTERED * (b.value + b.k // 6 + 1))
                    if not apart:
                        sp.wait_ge(q_scatter[(b.k // 2) % 3], scattered)
                    elif b.is_number(0):
                        for q in range(3):
                            sp.wait_ge(q_scatter[q], SCATTERED * len(range(q, NC, 3)))
                    reached(sp, s_nin, before)
                    sp.dma_start(n_aggr[0:b.rows, b.slot(3)], sums).then_inc(q_aggr[b.slot(3)], 16)
                if (b := node(-1)) is not None:
                    load_x(b)
                if (b := node(0)) is not None and b.fixed and not apart:
                    set_to_zero(range(zero_parts_begun(b.k), zero_parts_begun(b.k + 1)))

            load_ends(EDGES.at_step(0)(0))
            first_chunks(step, 0)
            sp.dma_start(o_dst[:], dst_rows).then_inc(s_order_in, 16)
            for to, frm in EDGE_PARAMS:
                sp.dma_start(to, frm).then_inc(s_edge_param, 16)
            first_chunks(step, *range(1, LEAD - 1))
            with nc.allow_non_contiguous_dma(reason="vectors as columns"):
                for to, frm in NODE_PARAMS:
                    sp.dma_start(to, frm).then_inc(s_node_param, 16)
            sp.wait_ge(s_zeros, 1)
            set_to_zero(range(zero_parts_begun(-1)))
            first_chunks(step, LEAD - 1)
            set_to_zero(range(zero_parts_begun(-1), zero_parts_begun(0)))
            branch(sp, 0, SP_LAG, step)
            for q in range(2):
                sp.wait_ge(q_out[q], 16 * len(range(q, NB, 2)))

        @block.gpsimd
        def _(pool):
            nc.gpsimd.memset(ident[:], 0.0).then_inc(s_const, 1)
            nc.gpsimd.memset(later[:], 1.0).then_inc(s_const, 1)
            nc.gpsimd.memset(minus_half[:], -0.5).then_inc(s_const, 1)
            nc.gpsimd.iota(spare[:], [[P, J]], base=N, channel_multiplier=1,
                           allow_small_or_imprecise_dtypes=True).then_inc(s_const, 1)
            nc.gpsimd.iota(o_high_limit[:], [[0, 1]], base=N, channel_multiplier=-2 * BLOCK,
                           allow_small_or_imprecise_dtypes=True).then_inc(s_const, 1)
            nc.gpsimd.iota(o_low_limit[:], [[0, 1]], base=AGGR_ROWS - ZERO_ROWS, channel_multiplier=-ZERO_ROWS // 2,
                           allow_small_or_imprecise_dtypes=True).then_inc(s_const, 1)
            pool.wait_ge(s_const, 6)
            nc.gpsimd.affine_select(out=ident[:], in_=ident[:], compare_op=ALU.not_equal, fill=1.0,
                                    base=0, pattern=[[-1, P]], channel_multiplier=1).then_inc(s_const, 1)
            nc.gpsimd.affine_select(out=later[:, 0:P], in_=later[:, 0:P], compare_op=ALU.is_ge, fill=0.0,
                                    base=0, pattern=[[1, P]], channel_multiplier=-1).then_inc(s_const, 1)
            last_node, last_sum, bound = (pool.alloc_register(n) for n in ("last_node", "last_sum", "bound"))
            pool.reg_mov(last_node, N - 2)
            pool.reg_mov(last_sum, AGGR_ROWS - 2)

            def gather(c):
                r, s = c.rows, c.slot(3)
                pool.wait_ge(q_cols[s], 16 * (c.uses(3) + 1))
                reached(pool, s_erelu, c.at - 2)
                pool.reg_add(bound, last_node, 1)
                for j in range(J):
                    nc.gpsimd.indirect_dma_start(
                        out=e_x[0:r, s, j, :], out_offset=None, in_=x,
                        in_offset=bass.IndirectOffsetOnAxis(ap=e_cols[0:r, s, 0, j:j + 1], axis=0),
                        bounds_check=bound,
                    ).then_inc(q_gather[s], 16)

            LAST_ZEROED = LEAD + NODE_TURN - 1 - EDGE_LAG

            def step(node, edge, halves, apart):
                if (b := node(2)) is not None:
                    r = b.rows
                    pool.wait_ge(s_nz, b.at + 1)
                    nc.gpsimd.tensor_tensor(n_zg[0:r, b.slot(2)], n_z[0:r, b.slot(2)], g1e_row[0:r],
                                            ALU.mult).then_inc(s_nzg, 1)
                    pool.wait_ge(s_nzg, b.at + 1)
                    pool.wait_ge(q_aggr[b.slot(3)], 16 * (b.uses(3) + 1))
                    reached(pool, s_tin, b.at - 1)
                    nc.gpsimd.tensor_tensor(n_in[0:r, b.slot(2)], n_zg[0:r, b.slot(2)], n_aggr[0:r, b.slot(3)],
                                            ALU.add).then_inc(s_nin, 1)
                if (b := node(4)) is not None:
                    r, s = b.rows, b.slot(6)
                    pool.wait_ge(s_var2, b.at + 1)
                    nc.gpsimd.tensor_tensor(n_rstd2[0:r, s], n_var2[0:r, s], minus_half[0:r, 0:J],
                                            ALU.pow).then_inc(s_rstd2, 1)
                if (b := node(1)) is not None:
                    r, s = b.rows, b.slot(6)
                    pool.wait_ge(s_nvar, b.at + 1)
                    nc.gpsimd.tensor_tensor(n_rstd[0:r, s], n_var[0:r, s],
                                            minus_half[0:r].rearrange("p (a j) -> p a j", j=J),
                                            ALU.pow).then_inc(s_nrstd, 1)
                if 0 in halves and (c := edge(0)) is not None:
                    gather(c)
                if 0 in halves and (c := edge(2)) is not None:
                    r, s = c.rows, c.slot(3)
                    if c.is_number(0):
                        pool.wait_ge(s_edge_param, 16 * len(EDGE_PARAMS))
                    pool.wait_ge(q_attr[s], 16 * (c.uses(3) + 1))
                    reached(pool, s_esum, c.at - 2)
                    nc.gpsimd.tensor_tensor(e_attrb[0:r, s], e_attr[0:r, s], b1_row[0:r],
                                            ALU.add).then_inc(s_eattrb, 1)
                    pool.wait_ge(s_evar, c.at + 1)
                    nc.gpsimd.tensor_tensor(e_rstd[0:r, s], e_var[0:r, s, 1], minus_half[0:r, 0:J],
                                            ALU.pow).then_inc(s_erstd, 1)
                if 1 in halves and (c := edge(3)) is not None:
                    r, s = c.rows, c.slot(3)
                    pool.wait_ge(s_emerged, c.at + 1)
                    pool.wait_ge(s_eindex, c.at + 1)
                    if c.fixed and apart and c.k == 0:
                        for q in s_zeroed:
                            pool.wait_ge(q, 16)
                    if c.fixed and not apart and c.k < LAST_ZEROED:
                        for q in s_zeroed[zeroed_for(c.k - 1) if c.k else 0:zeroed_for(c.k)]:
                            pool.wait_ge(q, 16)
                    if c.fixed and not apart and c.k == LAST_ZEROED:
                        for q in s_zeroed[zeroed_for(c.k - 1):]:
                            pool.wait_ge(q, 16)
                    if not c.is_number(0):
                        pool.wait_ge(q_scatter[(c.k - 1) % 3], SCATTERED * (c.value + (c.k - 1) // 3 + 1))
                    pool.reg_add(bound, last_sum, 1)
                    for j in range(J):
                        nc.gpsimd.indirect_dma_start(
                            out=aggr, out_offset=bass.IndirectOffsetOnAxis(
                                ap=e_index[0:r, s, j:j + 1], axis=0),
                            in_=e_merged[0:r, s, j, :], in_offset=None,
                            bounds_check=bound, compute_op=ALU.add,
                        ).then_inc(q_scatter[s], 16)

            first_chunks(step, *range(LEAD))
            pool.wait_ge(s_scaled_params, 2)
            branch(pool, EDGE_LAG, 4, step)

        @block.scalar
        def _(act):
            def per_row(to, of, scale, shift, rows):
                for j in range(J):
                    last = nc.scalar.activation(to[0:rows, j, :], of[0:rows, j, :], ACT.Identity,
                                                scale=scale[0:rows, j:j + 1],
                                                bias=shift[0:rows, j:j + 1])
                return last

            def gelu(b, k):
                act.wait_ge(s_f, b.at * KF + (k + 1))
                if k == 0:
                    reached(act, s_fout, b.at)
                nc.scalar.activation(n_act[:, k, :, 0:b.rows], p_f[k % 2][:, :, 0:b.rows],
                                     ACT.Gelu, bias=bf1_col[:, k:k + 1]).then_inc(s_act, 1)

            def hidden(b):
                act.wait_ge(s_g, b.at + 1)
                reached(act, s_gout, b.at - 1)
                nc.scalar.activation(n_gT[:, b.slot(2), :, 0:b.rows], p_g[:, :, 0:b.rows], ACT.Relu,
                                     bias=bg1e_col[:, 0:1]).then_inc(s_gT, 1)

            def step(node, edge, halves, apart):
                for k in range(max(KF, J)):
                    if k < KF and (b := node(6)) is not None:
                        gelu(b, k)
                    if k < J and (b := node(2)) is not None:
                        if k == 0:
                            act.wait_ge(s_nrstd, b.at + 1)
                            reached(act, s_x2, b.at - 5)
                        r = b.rows
                        last = nc.scalar.activation(n_h[0:r, b.slot(6), k, :], n_relu[0:r, b.slot(3), k, :],
                                                    ACT.Identity, scale=n_rstd[0:r, b.slot(6), 0, k:k + 1])
                        if k == J - 1:
                            last.then_inc(s_nh, 1)
                    if k == 1 and (b := node(3)) is not None:
                        hidden(b)
                if (b := node(5)) is not None:
                    act.wait_ge(s_tz2, b.at + 1)
                    reached(act, s_f, (b.at - 1) * KF)
                    nc.scalar.activation(n_z2T[:, b.slot(2), :, 0:b.rows], p_z2[:, :, 0:b.rows], ACT.Identity,
                                         bias=b2_col[:, 0:1], scale=g2_col[:, 0:1]).then_inc(s_z2T, 1)
                if (b := node(2)) is not None:
                    act.wait_ge(s_tin, b.at + 1)
                    reached(act, s_g, b.at - 1)
                    nc.scalar.activation(n_inT[:, b.slot(2), :, 0:b.rows], p_in[:, :, 0:b.rows],
                                         ACT.Identity).then_inc(s_inT, 1)
                if 1 in halves and (c := edge(3)) is not None:
                    act.wait_ge(s_emm, c.at + 1)
                    if not (c.fixed and c.k < 3):
                        act.wait_ge(q_scatter[c.slot(3)], SCATTERED * c.uses(3))
                    nc.scalar.activation(e_merged[0:c.rows, c.slot(3)], p_merged[0:c.rows],
                                         ACT.Identity).then_inc(s_emerged, 1)
                if (b := node(4)) is not None:
                    act.wait_ge(s_shift2, b.at + 1)
                    reached(act, s_tz2, b.at - 1)
                    per_row(n_z2[:, b.slot(2)], n_x2[:, b.slot(3)], n_rstd2[:, b.slot(6)],
                            n_shift2[:, b.slot(6)], b.rows).then_inc(s_z2, 1)
                if (b := node(1)) is not None:
                    act.wait_ge(s_nshift, b.at + 1)
                    reached(act, s_nzg, b.at - 1)
                    per_row(n_z[:, b.slot(2)], n_relu[:, b.slot(3)], n_rstd[:, b.slot(6), 1],
                            n_shift[:, b.slot(6)], b.rows).then_inc(s_nz, 1)
                if 1 in halves and (c := edge(2)) is not None:
                    act.wait_ge(s_esum, c.at + 1)
                    reached(act, s_emm, c.at - 2)
                    nc.scalar.activation(e_msg[0:c.rows, c.slot(3)], e_sum[0:c.rows, c.slot(3)],
                                         ACT.Relu).then_inc(s_emsg, 1)

            first_chunks(step, *range(LEAD))
            act.wait_ge(s_bias, 1)
            branch(act, EDGE_LAG, 6, step)

        @block.vector
        def _(dve):
            nc.vector.memset(zeros[:], 0.0).then_inc(s_zeros, 1)
            nc.vector.memset(ones[:], 1.0).then_inc(s_ones, 1)
            nc.vector.memset(ones_col[:], 1.0).then_inc(s_ones, 1)
            nc.vector.memset(bias_rows[:], 0.0).then_inc(s_rows, 1)

            dve.wait_ge(s_order_in, 16)
            nc.vector.tensor_reduce(o_high[:], o_dst[:], mybir.AxisListType.X, ALU.max).then_inc(s_bounds, 1)
            nc.vector.tensor_reduce(o_low[:], o_dst[:], mybir.AxisListType.X, ALU.min).then_inc(s_bounds, 1)
            dve.wait_ge(s_bounds, 2)
            dve.wait_ge(s_const, 6)
            nc.vector.tensor_tensor(o_above[:], o_high[:], o_high_limit[:], ALU.is_ge).then_inc(s_order, 1)
            nc.vector.tensor_tensor(o_below[:], o_low[:], o_low_limit[:], ALU.is_lt).then_inc(s_order, 1)
            dve.wait_ge(s_order, 2)
            nc.vector.tensor_tensor(o_bad[:], o_above[:], o_below[:], ALU.add).then_inc(s_order, 1)
            dve.wait_ge(s_bad, 1)
            nc.vector.tensor_copy(o_flag[:], p_in[0:1, 0, 0:1]).then_inc(s_flag, 1)

            def prepare_parameters():
                dve.wait_ge(s_node_param, 16 * len(NODE_PARAMS))
                nc.vector.tensor_scalar(eps_col[:], eps_col[:], 1.0, None, ALU.add).then_inc(s_eps, 1)
                dve.wait_ge(s_eps, 1)
                nc.vector.tensor_scalar(b1e_col[:], b1_col[:], eps_col[:, 0:1], None, ALU.mult).then_inc(s_scaled_params, 1)
                nc.vector.tensor_scalar(g1e_row[:], g1_row[:], eps_col[:, 0:1], None, ALU.mult).then_inc(s_scaled_params, 1)
                nc.vector.tensor_copy(bias_part[:, 0], bias_row[:]).then_inc(s_part, 1)
                dve.wait_ge(s_part, 1)
                nc.vector.tensor_tensor(bias_rest[:], bias_row[:], bias_part[:, 0], ALU.subtract).then_inc(s_part, 1)
                dve.wait_ge(s_part, 2)
                nc.vector.tensor_copy(bias_part[:, 1], bias_rest[:]).then_inc(s_part, 1)
                dve.wait_ge(s_part, 3)
                nc.vector.tensor_tensor(bias_row[:], bias_rest[:], bias_part[:, 1], ALU.subtract).then_inc(s_part, 1)
                dve.wait_ge(s_part, 4)
                nc.vector.tensor_copy(bias_part[:, 2], bias_row[:]).then_inc(s_part, 1)
                dve.wait_ge(s_part, 5)
                dve.wait_ge(s_rows, 1)
                for i in range(3):
                    for j in range(J):
                        last = nc.vector.tensor_copy(bias_rows[32 * i:32 * i + 1, :, j, :],
                                                     bias_part[32 * i:32 * i + 1, i])
                last.then_inc(s_rows, 1)
                dve.wait_ge(s_b1g, 1)
                nc.vector.tensor_tensor(bg1e_col[:], p_g[:, 0, 0:1], bg1_col[:], ALU.add).then_inc(s_bias, 1)

            dve.wait_ge(s_const, 8)

            def stats(to, of, rows, done):
                for j in range(J):
                    last = nc.vector.bn_stats(to[0:rows, j, :], of[0:rows, j, :])
                last.then_inc(done, 1)

            def moments(to, of, rows, done):
                for j in range(J):
                    last = nc.vector.bn_aggr(to[0:rows, j, :], of[0:rows, j, :])
                last.then_inc(done, 1)

            def centred_relu(to, of, mom, rows, done):
                for j in range(J):
                    last = nc.vector.tensor_scalar(to[0:rows, j, :], of[0:rows, j, :], mom[0:rows, j, 0:1],
                                                   0.0, ALU.subtract, ALU.max)
                last.then_inc(done, 1)

            def first_variance(var, mom, rows, done):
                nc.vector.tensor_scalar(var[0:rows, 0, :], mom[0:rows, 0, :, 1], EPS, None, ALU.add).then_inc(done, 1)

            def second_variance(var, mom, rows, first, at, done):
                dve.wait_ge(first, at + 1)
                nc.vector.scalar_tensor_tensor(var[0:rows, 1, :], var[0:rows, 0, :], EPS,
                                               mom[0:rows, 1, :, 1], ALU.mult, ALU.add).then_inc(done, 1)

            def shift(node):
                if (b := node(1)) is not None:
                    r, s = b.rows, b.slot(6)
                    dve.wait_ge(s_nrstd, b.at + 1)
                    nc.vector.scalar_tensor_tensor(n_shift[0:r, s], n_mom[0:r, s, 1, :, 0], -1.0, n_rstd[0:r, s, 1],
                                                   ALU.mult, ALU.mult).then_inc(s_nshift, 1)

            def shift2(node):
                if (b := node(4)) is not None:
                    r, s = b.rows, b.slot(6)
                    dve.wait_ge(s_rstd2, b.at + 1)
                    nc.vector.scalar_tensor_tensor(n_shift2[0:r, s], n_mom2[0:r, s, :, 0], -1.0, n_rstd2[0:r, s],
                                                   ALU.mult, ALU.mult).then_inc(s_shift2, 1)

            def relu_stats(node):
                if (b := node(0)) is not None:
                    dve.wait_ge(s_nrelu, b.at + 1)
                    stats(n_stat[:, b.slot(6), 1], n_relu[:, b.slot(3)], b.rows, s_nstatu)

            def relu_stats_done(node):
                if (b := node(0)) is not None:
                    dve.wait_ge(s_nstatu, b.at + 1)

            def relu_moments(node):
                if (b := node(0)) is not None:
                    moments(n_mom[:, b.slot(6), 1], n_stat[:, b.slot(6), 1], b.rows, s_nmomu)

            def variances_of(node, between=nothing):
                if (b := node(0)) is not None:
                    dve.wait_ge(s_nmomu, b.at + 1)
                    first_variance(n_var[:, b.slot(6)], n_mom[:, b.slot(6)], b.rows, s_nvar0)
                between(node)
                if b is not None:
                    second_variance(n_var[:, b.slot(6)], n_mom[:, b.slot(6)], b.rows, s_nvar0, b.at, s_nvar)

            def first_half(c, node):
                if c is not None:
                    s, r = c.slot(3), c.rows
                    dve.wait_ge(q_gather[s], 16 * J * (c.uses(3) + 1))
                    stats(e_stat[:, s, 0], e_x[:, s], r, s_estat)
                relu_stats(node)
                if c is not None:
                    dve.wait_ge(s_estat, c.at + 1)
                    nc.vector.tensor_copy(e_dstf[0:r, s], e_cols[0:r, s, 1, :]).then_inc(s_ecopy, 1)
                    moments(e_mom[:, s, 0], e_stat[:, s, 0], r, s_emom)
                    dve.wait_ge(s_ecopy, c.at + 1)
                    nc.vector.tensor_tensor(e_toward[0:r, s], spare[0:r], e_dstf[0:r, s],
                                            ALU.subtract).then_inc(s_etoward, 1)
                    dve.wait_ge(s_emom, c.at + 1)
                    centred_relu(e_relu[:, s], e_x[:, s], e_mom[:, s, 0], r, s_erelu)
                relu_stats_done(node)
                shift2(node)
                shift(node)
                relu_moments(node)
                if c is not None:
                    dve.wait_ge(q_dst[s], 16 * (c.uses(3) + 1))
                    reached(dve, s_emm, c.at - 2)
                    for a in range(J):
                        w = (J - a) * P
                        last = nc.vector.scalar_tensor_tensor(
                            e_match[0:r, s, MATCH_AT[a]:MATCH_AT[a] + w], e_dst[0:r, s, a * P:BLOCK],
                            e_dstf[0:r, s, a:a + 1], later[0:r, 0:w], ALU.is_equal, ALU.mult,
                            accum_out=e_count[0:r, s, a:a + 1])
                    last.then_inc(s_ematch, 1)
                variances_of(node)

            def second_half(c, ending, node):
                if c is not None:
                    s, r = c.slot(3), c.rows
                    dve.wait_ge(s_erelu, c.at + 1)
                    stats(e_stat[:, s, 1], e_relu[:, s], r, s_estatu)
                relu_stats(node)
                if c is not None:
                    dve.wait_ge(s_ematch, c.at + 1)
                    dve.wait_ge(s_etoward, c.at + 1)
                    dve.wait_ge(s_estatu, c.at + 1)
                    nc.vector.scalar_tensor_tensor(e_extra[0:r, s], e_count[0:r, s], 1.5, e_toward[0:r, s],
                                                   ALU.is_gt, ALU.mult).then_inc(s_eextra, 1)
                    moments(e_mom[:, s, 1], e_stat[:, s, 1], r, s_emomu)
                    if not (c.fixed and c.k < 3):
                        dve.wait_ge(q_scatter[s], SCATTERED * c.uses(3))
                    dve.wait_ge(s_eextra, c.at + 1)
                    nc.vector.tensor_tensor(e_index[0:r, s], e_dstf[0:r, s], e_extra[0:r, s],
                                            ALU.add).then_inc(s_eindex, 1)
                    dve.wait_ge(s_emomu, c.at + 1)
                    first_variance(e_var[:, s], e_mom[:, s], r, s_evar0)
                relu_stats_done(node)
                shift2(node)
                relu_moments(node)
                if c is not None:
                    second_variance(e_var[:, s], e_mom[:, s], r, s_evar0, c.at, s_evar)
                    if c.is_number(0):
                        dve.wait_ge(s_edge_param, 16 * len(EDGE_PARAMS))
                    for j in range(J):
                        last = nc.vector.scalar_tensor_tensor(
                            e_scaled[0:r, s, j, :], e_relu[0:r, s, j, :], e_mom[0:r, s, 1, j, 0:1],
                            g1_row[0:r, j, :], ALU.subtract, ALU.mult)
                    last.then_inc(s_escaled, 1)
                variances_of(node, shift)
                if ending is not None:
                    s, r = ending.slot(3), ending.rows
                    dve.wait_ge(s_escaled, ending.at + 1)
                    dve.wait_ge(s_erstd, ending.at + 1)
                    dve.wait_ge(s_eattrb, ending.at + 1)
                    reached(dve, s_emsg, ending.at - 2)
                    for j in range(J):
                        last = nc.vector.scalar_tensor_tensor(
                            e_sum[0:r, s, j, :], e_scaled[0:r, s, j, :], e_rstd[0:r, s, j:j + 1],
                            e_attrb[0:r, s, j, :], ALU.mult, ALU.add)
                    last.then_inc(s_esum, 1)

            def step(node, edge, halves, apart):
                first, fifth = node(0), node(4)
                if (b := fifth) is not None:
                    r, s = b.rows, b.slot(6)
                    dve.wait_ge(s_gout, b.at + 1)
                    dve.wait_ge(s_nh, b.at + 1)
                    reached(dve, s_z2, b.at - 2)
                    nc.vector.tensor_tensor(n_x2[0:r, b.slot(3)], p_gout[0:r], n_h[0:r, s],
                                            ALU.add).then_inc(s_x2, 1)
                if (b := first) is not None:
                    dve.wait_ge(q_x[b.slot(6)], 16 * (b.uses(6) + 1))
                    stats(n_stat[:, b.slot(6), 0], n_x[:, b.slot(6)], b.rows, s_nstat)
                if (b := node(7)) is not None:
                    r = b.rows
                    dve.wait_ge(s_fout, b.at + 1)
                    if not (b.fixed and b.k < 2):
                        dve.wait_ge(q_out[b.slot(2)], 16 * b.uses(2))
                    nc.vector.tensor_tensor(n_out[0:r, b.slot(2)], p_out[0:r], n_x2b[0:r, b.slot(6)],
                                            ALU.add).then_inc(s_nout, 1)
                if (b := first) is not None:
                    dve.wait_ge(s_nstat, b.at + 1)
                if (b := fifth) is not None:
                    dve.wait_ge(s_x2, b.at + 1)
                    stats(n_stat2[:, b.slot(6)], n_x2[:, b.slot(3)], b.rows, s_stat2)
                if (b := first) is not None:
                    moments(n_mom[:, b.slot(6), 0], n_stat[:, b.slot(6), 0], b.rows, s_nmom)
                if (b := fifth) is not None:
                    r, s = b.rows, b.slot(6)
                    dve.wait_ge(s_stat2, b.at + 1)
                    nc.vector.tensor_tensor(n_x2b[0:r, s], n_x2[0:r, b.slot(3)], n_x[0:r, s],
                                            ALU.add).then_inc(s_x2b, 1)
                    moments(n_mom2[:, s], n_stat2[:, s], r, s_mom2)
                if (b := first) is not None:
                    dve.wait_ge(s_nmom, b.at + 1)
                    reached(dve, s_nh, b.at - 2)
                    centred_relu(n_relu[:, b.slot(3)], n_x[:, b.slot(6)], n_mom[:, b.slot(6), 0], b.rows, s_nrelu)
                if (b := fifth) is not None:
                    r, s = b.rows, b.slot(6)
                    dve.wait_ge(s_mom2, b.at + 1)
                    nc.vector.tensor_scalar(n_var2[0:r, s], n_mom2[0:r, s, :, 1], EPS, None,
                                            ALU.add).then_inc(s_var2, 1)
                if 0 in halves or not halves:
                    first_half(edge(1), node)
                if 1 in halves:
                    second_half(edge(1), edge(2), node)

            first_chunks(step, *range(LEAD))
            prepare_parameters()
            branch(dve, EDGE_LAG, NODE_LAG, step)

        @block.tensor
        def _(pe):
            pe.wait_ge(s_order, 3)
            pe.wait_ge(s_ones, 2)
            nc.tensor.matmul(p_in[0:1, 0, 0:1], o_bad[:], ones_col[0:NC, :], start=True, stop=True).then_inc(s_bad, 1)
            pe.wait_ge(s_scaled_params, 1)
            nc.tensor.matmul(p_g[:, 0, 0:1], wg1[:], b1e_col[:], start=True, stop=True).then_inc(s_b1g, 1)
            pe.wait_ge(s_bias, 1)
            pe.wait_ge(s_const, 8)
            pe.wait_ge(s_rows, 2)

            def add_bias(to, which):
                nc.tensor.matmul(to[:], ones[:], bias_rows[:, which], start=True, stop=False,
                                 skip_group_check=True)

            def first_product(b, ks):
                for k in ks:
                    reached(pe, s_act, b.at * KF + k - 1)
                    nc.tensor.matmul(p_f[k % 2][:, :, 0:b.rows], wf1[:, k * P:(k + 1) * P],
                                     n_z2T[:, b.slot(2), :, 0:b.rows], start=True, stop=True).then_inc(s_f, 1)

            def step(node, edge, halves, apart):
                third, fourth, sixth, seventh = node(2), node(3), node(5), node(6)
                if (b := seventh) is not None:
                    pe.wait_ge(s_z2T, b.at + 1)
                    first_product(b, (0, 1))
                if (b := fourth) is not None:
                    pe.wait_ge(s_inT, b.at + 1)
                    reached(pe, s_gT, b.at)
                    nc.tensor.matmul(p_g[:, :, 0:b.rows], wg1[:], n_inT[:, b.slot(2), :, 0:b.rows],
                                     start=True, stop=True).then_inc(s_g, 1)
                if (b := seventh) is not None:
                    first_product(b, (2, 3))
                if (b := fourth) is not None:
                    reached(pe, s_x2, b.at)
                    add_bias(p_gout, 0)
                    pe.wait_ge(s_gT, b.at + 1)
                    for j in range(J):
                        last = nc.tensor.matmul(p_gout[0:b.rows, j, :], n_gT[:, b.slot(2), j, 0:b.rows], wg2[:],
                                                start=False, stop=True, skip_group_check=True)
                    last.then_inc(s_gout, 1)
                if (b := sixth) is not None:
                    pe.wait_ge(s_z2, b.at + 1)
                    reached(pe, s_z2T, b.at)
                    for j in range(J):
                        last = nc.tensor.transpose(p_z2[:, j, 0:b.rows], n_z2[0:b.rows, b.slot(2), j, :],
                                                   ident[0:b.rows, 0:b.rows])
                    last.then_inc(s_tz2, 1)
                if (b := third) is not None:
                    pe.wait_ge(s_nin, b.at + 1)
                    reached(pe, s_inT, b.at)
                    for j in range(J):
                        last = nc.tensor.transpose(p_in[:, j, 0:b.rows], n_in[0:b.rows, b.slot(2), j, :],
                                                   ident[0:b.rows, 0:b.rows])
                    last.then_inc(s_tin, 1)
                if (b := seventh) is not None:
                    reached(pe, s_nout, b.at)
                    add_bias(p_out, 1)
                    for k in range(KF):
                        pe.wait_ge(s_act, b.at * KF + (k + 1))
                        for j in range(J):
                            last = nc.tensor.matmul(p_out[0:b.rows, j, :], n_act[:, k, j, 0:b.rows], wf2[:, k, :],
                                                    start=False, stop=(k == KF - 1), skip_group_check=True)
                    last.then_inc(s_fout, 1)
                if 0 in halves and (c := edge(3)) is not None:
                    s, r = c.slot(3), c.rows
                    pe.wait_ge(s_ematch, c.at + 1)
                    pe.wait_ge(s_emsg, c.at + 1)
                    reached(pe, s_emerged, c.at)
                    for i in range(J):
                        for a in range(i + 1):
                            m = MATCH_AT[a] + (i - a) * P
                            last = nc.tensor.matmul(p_merged[0:r, i, :], e_match[0:r, s, m:m + r],
                                                    e_msg[0:r, s, a, :], start=(a == 0), stop=(a == i))
                    last.then_inc(s_emm, 1)

            branch(pe, EDGE_LAG, 6, step)


_WEIGHTS = ["g1", "b1", "g2", "b2", "eps_gin", "Wg1", "bg1", "Wg2", "bg2", "Wf1", "bf1", "Wf2", "bf2"]


def kernel(**inputs):
    import numpy as _np
    import concourse.bacc as _bacc
    from concourse import mybir as _mybir
    from concourse.bass_utils import run_bass_kernel_spmd as _run

    x = _np.ascontiguousarray(inputs["x"])
    attr = _np.ascontiguousarray(inputs["edge_attr_128"])
    edges = attr.shape[0]
    short = edges % BLOCK

    def in_chunks(a, fill):
        a = _np.asarray(a)
        first = _np.pad(a[:short], (0, BLOCK - short), constant_values=fill).reshape(1, BLOCK)
        return _np.concatenate([a[short:].reshape(-1, BLOCK)[::-1], first]).reshape(-1, P, J)

    src, dst = in_chunks(inputs["src"], 0), in_chunks(inputs["dst"], -1)
    arrays = {"in_x": x, "in_attr": attr,
              "in_edge_cols": _np.ascontiguousarray(_np.stack([src, dst], 2).reshape(-1, 2 * J)),
              "in_dst_rows": _np.ascontiguousarray(dst.transpose(0, 2, 1).reshape(-1, BLOCK))}
    for name in _WEIGHTS:
        arrays[f"in_{name}"] = _np.ascontiguousarray(inputs[f"L0_gnn_{name}"])
    arrays["in_eps_gin"] = arrays["in_eps_gin"].reshape(1)

    nc = _bacc.Bacc("TRN2", target_bir_lowering=False, num_devices=1)
    args = [nc.dram_tensor(n, a.shape, _mybir.dt.from_np(a.dtype), kind="ExternalInput").ap()
            for n, a in arrays.items()]
    out = nc.dram_tensor("out_dram", x.shape, _mybir.dt.float32, kind="ExternalOutput").ap()
    gnn_kernel(nc, *args, out)
    r = _run(nc, [arrays], core_ids=[0])
    return r.results[0]["out_dram"]
```
